# Optimizing a Trainium2 kernel written in Bass

```python
import numpy as np
import jax
import jax.numpy as jnp

def _softmax(x, axis=-1):
    return jax.nn.softmax(x, axis=axis)
def _gelu(x):
    return jax.nn.gelu(x, approximate=True)
def _silu(x):
    return jax.nn.silu(x)
def _sigmoid(x):
    return jax.nn.sigmoid(x)
def _layernorm(x, axis=-1, eps=1e-5):
    m = jnp.mean(x, axis=axis, keepdims=True)
    v = jnp.var(x, axis=axis, keepdims=True)
    return (x - m) / jnp.sqrt(v + eps)
def _scatter_add(tgt, idx, src, axis=0):
    return tgt.at[idx].add(src)
def _segment_sum(src, seg, n):
    return jax.ops.segment_sum(src, seg, n)

kernel_name = 'mk_conv_preact_d4_conv_nchw256_6ca2ab'

def setup_inputs(seed: int = 0):
    np.random.seed(seed)
    _w = jnp.asarray
    def _rec_inputs():
        import jax
        import jax.numpy as jnp
        _gk = jax.random.key(seed)
        x = 7.22e-05 + 1 * jax.random.normal(jax.random.fold_in(_gk, 1), (8, 256, 64, 64), jnp.float32)
        return x
    x = _rec_inputs()
    def _L0_conv_setup():
        import jax, jax.numpy as jnp
        import numpy as np
        from jax import lax
        EPS = 1e-05

        def _zpool(x):
            return jnp.concatenate([x.max(axis=1, keepdims=True), x.mean(axis=1, keepdims=True)], axis=1)

        def _gate(x, w, g, b, m, v):
            z = _zpool(x)
            y = lax.conv_general_dilated(z, w, (1, 1), [(3, 3), (3, 3)], dimension_numbers=('NCHW', 'OIHW', 'NCHW'))
            scale = g / jnp.sqrt(v + EPS)
            y = (y - m[None, :, None, None]) * scale[None, :, None, None] + b[None, :, None, None]
            return x * jax.nn.sigmoid(y)
        key = jax.random.key(seed)
        ks = jax.random.split(key, 8)
        B, C, H, W = (8, 256, 64, 64)
        inp = {'x': jax.random.normal(ks[0], (B, C, H, W), dtype=jnp.float32), 'w_cw': jax.random.normal(ks[1], (1, 2, 7, 7), dtype=jnp.float32) * 0.1, 'g_cw': jnp.ones((1,), jnp.float32), 'b_cw': jnp.zeros((1,), jnp.float32), 'm_cw': jnp.zeros((1,), jnp.float32), 'v_cw': jnp.ones((1,), jnp.float32), 'w_hc': jax.random.normal(ks[2], (1, 2, 7, 7), dtype=jnp.float32) * 0.1, 'g_hc': jnp.ones((1,), jnp.float32), 'b_hc': jnp.zeros((1,), jnp.float32), 'm_hc': jnp.zeros((1,), jnp.float32), 'v_hc': jnp.ones((1,), jnp.float32), 'w_hw': jax.random.normal(ks[3], (1, 2, 7, 7), dtype=jnp.float32) * 0.1, 'g_hw': jnp.ones((1,), jnp.float32), 'b_hw': jnp.zeros((1,), jnp.float32), 'm_hw': jnp.zeros((1,), jnp.float32), 'v_hw': jnp.ones((1,), jnp.float32), 'w1d': jax.random.normal(ks[4], (3, 1, 7), dtype=jnp.float32) * 0.1}
        return inp
    _L0_conv_all = _L0_conv_setup()
    _L0_conv_in = {k: v for k, v in _L0_conv_all.items() if k in ('w_cw', 'g_cw', 'b_cw', 'm_cw', 'v_cw', 'w_hc', 'g_hc', 'b_hc', 'm_hc', 'v_hc', 'w_hw', 'g_hw', 'b_hw', 'm_hw', 'v_hw', 'w1d', )}
    del _L0_conv_all

    def _L1_conv_setup():
        import jax, jax.numpy as jnp
        import numpy as np
        IN_F, OUT_F, K, STRIDE, PAD = (256, 256, 3, 1, 1)
        SEARCH_SPACE = (2, 4, 8, 16)

        def _cir_project(weight, b):
            q, p = (OUT_F // b, IN_F // b)
            tmp = weight.reshape(q, b, p, b, K, K).transpose(0, 2, 1, 3, 4, 5)
            j = jnp.arange(b)
            diag_idx = (j[:, None] + j[None, :]) % b
            tc = tmp[:, :, j[:, None], diag_idx].mean(axis=2)
            circ_idx = (j[:, None] - j[None, :]) % b
            w = tc[:, :, circ_idx]
            return w.transpose(0, 2, 1, 3, 4, 5).reshape(OUT_F, IN_F, K, K)
        key = jax.random.key(seed)
        k1, k2 = jax.random.split(key, 2)
        x = jax.random.normal(k1, (256, IN_F, 16, 16), jnp.float32)
        weight = jax.random.normal(k2, (OUT_F, IN_F, K, K), jnp.float32) * 0.05
        alphas = jnp.ones((len(SEARCH_SPACE) + 1,), jnp.float32)
        return {'x': x, 'weight': weight, 'alphas': alphas}
    _L1_conv_all = _L1_conv_setup()
    _L1_conv_in = {k: v for k, v in _L1_conv_all.items() if k in ('weight', 'alphas', )}
    del _L1_conv_all

    def _L2_conv_setup():
        import jax, jax.numpy as jnp
        import numpy as np
        DB8_DEC_LO = jnp.array([-0.00011747678400228192, 0.0006754494059985568, -0.0003917403729959771, -0.00487035299301066, 0.008746094047015655, 0.013981027917015516, -0.04408825393106472, -0.01736930100202211, 0.128747426620186, 0.00047248457399797254, -0.2840155429624281, -0.015829105256023893, 0.5853546836548691, 0.6756307362980128, 0.3128715909144659, 0.05441584224308161], dtype=jnp.float32)

        def _dwt_lo_last(x, filt):
            flen = filt.shape[0]
            pad = [(0, 0)] * (x.ndim - 1) + [(flen - 1, flen - 1)]
            xe = jnp.pad(x, pad, mode='symmetric')[..., 1:]
            lead = x.shape[:-1]
            y = jax.lax.conv_general_dilated(xe.reshape(int(np.prod(lead)), 1, xe.shape[-1]), filt[::-1].reshape(1, 1, flen), window_strides=(2,), padding='VALID')
            return y.reshape(*lead, -1)

        def dwt2_ll(x, filt):
            y = _dwt_lo_last(x, filt)
            y = jnp.swapaxes(y, -1, -2)
            y = _dwt_lo_last(y, filt)
            return jnp.swapaxes(y, -1, -2)
        key = jax.random.key(seed)
        k1, k2, k3 = jax.random.split(key, 3)
        B, C, H, W = (8, 256, 256, 256)
        r = 16
        x = jax.random.normal(k1, (B, C, H, W), dtype=jnp.float32)
        W1 = jax.random.normal(k2, (C // r, C), dtype=jnp.float32) * (1.0 / np.sqrt(C))
        W2 = jax.random.normal(k3, (C, C // r), dtype=jnp.float32) * (1.0 / np.sqrt(C // r))
        return {'x': x, 'W1': W1, 'W2': W2}
    _L2_conv_all = _L2_conv_setup()
    _L2_conv_in = {k: v for k, v in _L2_conv_all.items() if k in ('W1', 'W2', )}
    del _L2_conv_all

    def _L3_conv_setup():
        import jax, jax.numpy as jnp
        import numpy as np
        WS = 8
        SHIFT = WS // 2
        HEADS = 8

        def _rel_pos_index(ws):
            coords = np.stack(np.meshgrid(np.arange(ws), np.arange(ws), indexing='ij'), 0).reshape(2, -1)
            rel = coords[:, :, None] - coords[:, None, :]
            rel = rel.transpose(1, 2, 0) + (ws - 1)
            return rel[..., 0] * (2 * ws - 1) + rel[..., 1]

        def _shift_mask(H, W, ws, shift):
            img = np.zeros((H, W), dtype=np.int32)
            cnt = 0
            for hs in (slice(0, -ws), slice(-ws, -shift), slice(-shift, None)):
                for wsl in (slice(0, -ws), slice(-ws, -shift), slice(-shift, None)):
                    img[hs, wsl] = cnt
                    cnt += 1
            mw = img.reshape(H // ws, ws, W // ws, ws).transpose(0, 2, 1, 3).reshape(-1, ws * ws)
            diff = mw[:, None, :] - mw[:, :, None]
            return np.where(diff != 0, -100.0, 0.0).astype(np.float32)
        key = jax.random.key(seed)
        ks = jax.random.split(key, 6)
        B, C, H, W = (32, 256, 64, 64)
        return {'x': jax.random.normal(ks[0], (B, C, H, W), jnp.float32), 'w_qkv': jax.random.normal(ks[1], (C, 3 * C), jnp.float32) * C ** (-0.5), 'b_qkv': jnp.zeros((3 * C,), jnp.float32), 'w_o': jax.random.normal(ks[2], (C, C), jnp.float32) * C ** (-0.5), 'b_o': jnp.zeros((C,), jnp.float32), 'rel_bias_table': jax.random.normal(ks[3], ((2 * WS - 1) ** 2, HEADS), jnp.float32) * 0.02}
    _L3_conv_all = _L3_conv_setup()
    _L3_conv_in = {k: v for k, v in _L3_conv_all.items() if k in ('w_qkv', 'b_qkv', 'w_o', 'b_o', 'rel_bias_table', )}
    del _L3_conv_all

    return {
        "x": x,
        "L0_conv_w_cw": _L0_conv_in["w_cw"],
        "L0_conv_g_cw": _L0_conv_in["g_cw"],
        "L0_conv_b_cw": _L0_conv_in["b_cw"],
        "L0_conv_m_cw": _L0_conv_in["m_cw"],
        "L0_conv_v_cw": _L0_conv_in["v_cw"],
        "L0_conv_w_hc": _L0_conv_in["w_hc"],
        "L0_conv_g_hc": _L0_conv_in["g_hc"],
        "L0_conv_b_hc": _L0_conv_in["b_hc"],
        "L0_conv_m_hc": _L0_conv_in["m_hc"],
        "L0_conv_v_hc": _L0_conv_in["v_hc"],
        "L0_conv_w_hw": _L0_conv_in["w_hw"],
        "L0_conv_g_hw": _L0_conv_in["g_hw"],
        "L0_conv_b_hw": _L0_conv_in["b_hw"],
        "L0_conv_m_hw": _L0_conv_in["m_hw"],
        "L0_conv_v_hw": _L0_conv_in["v_hw"],
        "L0_conv_w1d": _L0_conv_in["w1d"],
        "L1_conv_weight": _L1_conv_in["weight"],
        "L1_conv_alphas": _L1_conv_in["alphas"],
        "L2_conv_W1": _L2_conv_in["W1"],
        "L2_conv_W2": _L2_conv_in["W2"],
        "L3_conv_w_qkv": _L3_conv_in["w_qkv"],
        "L3_conv_b_qkv": _L3_conv_in["b_qkv"],
        "L3_conv_w_o": _L3_conv_in["w_o"],
        "L3_conv_b_o": _L3_conv_in["b_o"],
        "L3_conv_rel_bias_table": _L3_conv_in["rel_bias_table"],
    }

def reference(x, L0_conv_w_cw, L0_conv_g_cw, L0_conv_b_cw, L0_conv_m_cw, L0_conv_v_cw, L0_conv_w_hc, L0_conv_g_hc, L0_conv_b_hc, L0_conv_m_hc, L0_conv_v_hc, L0_conv_w_hw, L0_conv_g_hw, L0_conv_b_hw, L0_conv_m_hw, L0_conv_v_hw, L0_conv_w1d, L1_conv_weight, L1_conv_alphas, L2_conv_W1, L2_conv_W2, L3_conv_w_qkv, L3_conv_b_qkv, L3_conv_w_o, L3_conv_b_o, L3_conv_rel_bias_table):
    import jax
    import jax.numpy as jnp
    def _L0_conv_ref(x, w_cw, g_cw, b_cw, m_cw, v_cw, w_hc, g_hc, b_hc, m_hc, v_hc, w_hw, g_hw, b_hw, m_hw, v_hw, w1d):
        import jax, jax.numpy as jnp
        import numpy as np
        from jax import lax
        EPS = 1e-05

        def _zpool(x):
            return jnp.concatenate([x.max(axis=1, keepdims=True), x.mean(axis=1, keepdims=True)], axis=1)

        def _gate(x, w, g, b, m, v):
            z = _zpool(x)
            y = lax.conv_general_dilated(z, w, (1, 1), [(3, 3), (3, 3)], dimension_numbers=('NCHW', 'OIHW', 'NCHW'))
            scale = g / jnp.sqrt(v + EPS)
            y = (y - m[None, :, None, None]) * scale[None, :, None, None] + b[None, :, None, None]
            return x * jax.nn.sigmoid(y)
        b1 = _gate(x.transpose(0, 2, 1, 3), w_cw, g_cw, b_cw, m_cw, v_cw).transpose(0, 2, 1, 3)
        b2 = _gate(x.transpose(0, 3, 2, 1), w_hc, g_hc, b_hc, m_hc, v_hc).transpose(0, 3, 2, 1)
        b3 = _gate(x, w_hw, g_hw, b_hw, m_hw, v_hw)
        x_out = (b1 + b2 + b3) / 3.0
        pooled = x_out.mean(axis=(2, 3))
        logits = lax.conv_general_dilated(pooled[:, None, :], w1d, (1,), [(3, 3)], dimension_numbers=('NCH', 'OIH', 'NCH'))
        wts = jax.nn.softmax(logits, axis=1)[..., None, None]
        branches = jnp.stack([b1, b2, b3], axis=1)
        return (wts * branches).sum(axis=1)

    def _L1_conv_ref(x, weight, alphas):
        import jax, jax.numpy as jnp
        import numpy as np
        IN_F, OUT_F, K, STRIDE, PAD = (256, 256, 3, 1, 1)
        SEARCH_SPACE = (2, 4, 8, 16)

        def _cir_project(weight, b):
            q, p = (OUT_F // b, IN_F // b)
            tmp = weight.reshape(q, b, p, b, K, K).transpose(0, 2, 1, 3, 4, 5)
            j = jnp.arange(b)
            diag_idx = (j[:, None] + j[None, :]) % b
            tc = tmp[:, :, j[:, None], diag_idx].mean(axis=2)
            circ_idx = (j[:, None] - j[None, :]) % b
            w = tc[:, :, circ_idx]
            return w.transpose(0, 2, 1, 3, 4, 5).reshape(OUT_F, IN_F, K, K)
        a = jax.nn.softmax(alphas)
        w = a[0] * weight
        for i, b in enumerate(SEARCH_SPACE):
            w = w + a[i + 1] * _cir_project(weight, b)
        return jax.lax.conv_general_dilated(x, w, window_strides=(STRIDE, STRIDE), padding=[(PAD, PAD), (PAD, PAD)], dimension_numbers=('NCHW', 'OIHW', 'NCHW'))

    def _L2_conv_ref(x, W1, W2):
        import jax, jax.numpy as jnp
        import numpy as np
        DB8_DEC_LO = jnp.array([-0.00011747678400228192, 0.0006754494059985568, -0.0003917403729959771, -0.00487035299301066, 0.008746094047015655, 0.013981027917015516, -0.04408825393106472, -0.01736930100202211, 0.128747426620186, 0.00047248457399797254, -0.2840155429624281, -0.015829105256023893, 0.5853546836548691, 0.6756307362980128, 0.3128715909144659, 0.05441584224308161], dtype=jnp.float32)

        def _dwt_lo_last(x, filt):
            flen = filt.shape[0]
            pad = [(0, 0)] * (x.ndim - 1) + [(flen - 1, flen - 1)]
            xe = jnp.pad(x, pad, mode='symmetric')[..., 1:]
            lead = x.shape[:-1]
            y = jax.lax.conv_general_dilated(xe.reshape(int(np.prod(lead)), 1, xe.shape[-1]), filt[::-1].reshape(1, 1, flen), window_strides=(2,), padding='VALID')
            return y.reshape(*lead, -1)

        def dwt2_ll(x, filt):
            y = _dwt_lo_last(x, filt)
            y = jnp.swapaxes(y, -1, -2)
            y = _dwt_lo_last(y, filt)
            return jnp.swapaxes(y, -1, -2)
        ll = dwt2_ll(x, DB8_DEC_LO)
        y = jnp.mean(ll, axis=(2, 3))
        h = jax.nn.relu(y @ W1.T)
        w = jax.nn.sigmoid(h @ W2.T)
        return x * w[:, :, None, None]

    def _L3_conv_ref(x, w_qkv, b_qkv, w_o, b_o, rel_bias_table):
        import jax, jax.numpy as jnp
        import numpy as np
        WS = 8
        SHIFT = WS // 2
        HEADS = 8

        def _rel_pos_index(ws):
            coords = np.stack(np.meshgrid(np.arange(ws), np.arange(ws), indexing='ij'), 0).reshape(2, -1)
            rel = coords[:, :, None] - coords[:, None, :]
            rel = rel.transpose(1, 2, 0) + (ws - 1)
            return rel[..., 0] * (2 * ws - 1) + rel[..., 1]

        def _shift_mask(H, W, ws, shift):
            img = np.zeros((H, W), dtype=np.int32)
            cnt = 0
            for hs in (slice(0, -ws), slice(-ws, -shift), slice(-shift, None)):
                for wsl in (slice(0, -ws), slice(-ws, -shift), slice(-shift, None)):
                    img[hs, wsl] = cnt
                    cnt += 1
            mw = img.reshape(H // ws, ws, W // ws, ws).transpose(0, 2, 1, 3).reshape(-1, ws * ws)
            diff = mw[:, None, :] - mw[:, :, None]
            return np.where(diff != 0, -100.0, 0.0).astype(np.float32)
        B, C, H, W = x.shape
        ws, shift, heads = (WS, SHIFT, HEADS)
        dh = C // heads
        nH, nW = (H // ws, W // ws)
        nWin, N = (nH * nW, ws * ws)
        rel_idx = jnp.asarray(_rel_pos_index(ws))
        mask = jnp.asarray(_shift_mask(H, W, ws, shift))
        xs = jnp.roll(x, (-shift, -shift), axis=(2, 3))
        xw = xs.reshape(B, C, nH, ws, nW, ws).transpose(0, 2, 4, 3, 5, 1).reshape(B, nWin, N, C)
        qkv = xw @ w_qkv + b_qkv
        qkv = qkv.reshape(B, nWin, N, 3, heads, dh)
        q = qkv[..., 0, :, :].transpose(0, 1, 3, 2, 4)
        k = qkv[..., 1, :, :].transpose(0, 1, 3, 2, 4)
        v = qkv[..., 2, :, :].transpose(0, 1, 3, 2, 4)
        attn = jnp.einsum('bwhnd,bwhmd->bwhnm', q, k) * dh ** (-0.5)
        bias = rel_bias_table[rel_idx]
        attn = attn + bias.transpose(2, 0, 1)[None, None]
        attn = attn + mask[None, :, None]
        attn = jax.nn.softmax(attn, axis=-1)
        out = jnp.einsum('bwhnm,bwhmd->bwhnd', attn, v)
        out = out.transpose(0, 1, 3, 2, 4).reshape(B, nWin, N, C)
        out = out @ w_o + b_o
        out = out.reshape(B, nH, nW, ws, ws, C).transpose(0, 5, 1, 3, 2, 4).reshape(B, C, H, W)
        return jnp.roll(out, (shift, shift), axis=(2, 3))

    def _gn(v, G=32, eps=1e-5):
        B_, C_, H_, W_ = v.shape
        g = v.reshape(B_, G, C_ // G, H_, W_)
        m = jnp.mean(g, axis=(2, 3, 4), keepdims=True)
        s = jnp.var(g, axis=(2, 3, 4), keepdims=True)
        return ((g - m) / jnp.sqrt(s + eps)).reshape(v.shape)

    def _ln_c(v, eps=1e-6):
        m = jnp.mean(v, axis=1, keepdims=True)
        s = jnp.var(v, axis=1, keepdims=True)
        return (v - m) / jnp.sqrt(s + eps)

    def _ln_t(v, eps=1e-5):
        m = jnp.mean(v, axis=-1, keepdims=True)
        s = jnp.var(v, axis=-1, keepdims=True)
        return (v - m) / jnp.sqrt(s + eps)

    def _to_tokens(v):
        B_, C_, H_, W_ = v.shape
        return v.reshape(B_, C_, H_ * W_).transpose(0, 2, 1)
    def _from_tokens(t, like):
        B_, C_, H_, W_ = like.shape
        return t.transpose(0, 2, 1).reshape(B_, C_, H_, W_)

    x = x + _L0_conv_ref(_gn(x), L0_conv_w_cw, L0_conv_g_cw, L0_conv_b_cw, L0_conv_m_cw, L0_conv_v_cw, L0_conv_w_hc, L0_conv_g_hc, L0_conv_b_hc, L0_conv_m_hc, L0_conv_v_hc, L0_conv_w_hw, L0_conv_g_hw, L0_conv_b_hw, L0_conv_m_hw, L0_conv_v_hw, L0_conv_w1d)
    x = x + _L1_conv_ref(_gn(x), L1_conv_weight, L1_conv_alphas)
    x = x + _L2_conv_ref(_gn(x), L2_conv_W1, L2_conv_W2)
    x = x + _L3_conv_ref(_gn(x), L3_conv_w_qkv, L3_conv_b_qkv, L3_conv_w_o, L3_conv_b_o, L3_conv_rel_bias_table)
    return x


_drawn_inputs = setup_inputs


def setup_inputs(seed=0):
    import zlib

    import numpy as np

    out = dict(_drawn_inputs(seed))
    spreads = {'L1_conv_alphas': (1.0, 0.6), 'L3_conv_b_qkv': (0.0, 0.1), 'L3_conv_b_o': (0.0, 0.1)}
    factors = {'L0_conv_w_hc': 200.0,
     'L0_conv_w1d': 183.646,
     'L2_conv_W1': 8.0,
     'L2_conv_W2': 8.0,
     'L3_conv_rel_bias_table': 33.324}
    for name, (base, spread) in spreads.items():
        noise = np.random.default_rng([zlib.crc32(name.encode()), seed]).standard_normal(out[name].shape)
        drawn = base * np.exp(spread * noise) if base else spread * noise
        out[name] = jnp.asarray(drawn.astype(out[name].dtype))
    for name, factor in factors.items():
        out[name] = (out[name] * factor).astype(out[name].dtype)
    return out
```

```python
import numpy as np

import concourse.bass as bass
from concourse import mybir
from contextlib import ExitStack

NB, C, H, W = 8, 256, 64, 64
P = 128
CT = C // P
HW = H * W
CHUNK = 512
NCH = HW // CHUNK
ROWS = CHUNK // W
KS = 7
PAD = KS // 2
BAND = P + 2 * PAD
NM = 2 * KS
PT = W + 2 * PAD
PAIRS = HW // P
DJ = 5
C3 = 3
TAPS = C3 * C3
HP = H + 2
BLOCKS = (2, 4, 8, 16)
BMAX = BLOCKS[-1]
HEADS, WS, SHIFT = 8, 8, 4
DH = C // HEADS
TOK = WS * WS
NW = W // WS
GROUP = 8
HID = C // 16
EPS = 1e-5
FULL = 256.0
T_CW, T_HW, T_1D = 0, 2 * NM * BAND, 2 * NM * BAND + 2 * DJ * 2 * PT
W1D = 3 * P
T_ALL = T_1D + 3 * W1D

DB8_LO = [-0.00011747678400228192, 0.0006754494059985568, -0.0003917403729959771, -0.00487035299301066,
          0.008746094047015655, 0.013981027917015516, -0.04408825393106472, -0.01736930100202211,
          0.128747426620186, 0.00047248457399797254, -0.2840155429624281, -0.015829105256023893,
          0.5853546836548691, 0.6756307362980128, 0.3128715909144659, 0.05441584224308161]


def dwt_mean_weights(n):
    taps = np.asarray(DB8_LO, np.float32).astype(np.float64)
    flen = len(taps)
    source = np.pad(np.arange(n), flen - 1, mode="symmetric")[1:]
    count = (n + flen - 1) // 2
    u = np.zeros(n)
    for m in range(count):
        for k in range(flen):
            u[source[2 * m + k]] += taps[flen - 1 - k] / count
    return u


def build(nc, x, k_cw, k_hc, k_hw, bn, k_1d, w_conv, alphas, w1t, w2t, w_qkv, b_qkv, w_o, b_o,
          rel_t, c_gavg, c_ident, c_ind, c_ones3, c_mask, c_u, c_half, out):
    fp32, fp16 = mybir.dt.float32, mybir.dt.float16
    ALU, ACT, AX = mybir.AluOpType, mybir.ActivationFunctionType, mybir.AxisListType
    ABSMAX = bass.bass_isa.ReduceOp.absmax
    u_sum = float(dwt_mean_weights(W).sum())
    V, S, T, G = nc.vector, nc.scalar, nc.tensor, nc.gpsimd
    ctx = ExitStack()
    with ctx:
        def sb(name, shape, dt=fp32):
            return ctx.enter_context(nc.sbuf_tensor(name, shape, dt))

        def ps(name, shape):
            return ctx.enter_context(nc.psum_tensor(name, shape, fp32))

        def sem(name):
            s = ctx.enter_context(nc.semaphore(name))
            sems.append(s)
            return s

        sems = []
        X = sb("X", [P, CT, HW])
        g_raw = sb("g_raw", [P, CT * 2 * HP * HP], fp16)
        Gn = g_raw[:, 0:CT * HW * 2].bitcast(fp32).rearrange("p (t n) -> p t n", t=CT)
        halves = g_raw[:, :].rearrange("p (l t r c) -> p l t r c", l=2, t=CT, r=HP)
        cw_hi = sb("cw_hi", [P, CT, TAPS, C], fp16)
        cw_lo = sb("cw_lo", [P, CT, TAPS, C], fp16)
        qkv_hi = sb("qkv_hi", [P, CT, 3 * C], fp16)
        qkv_lo = sb("qkv_lo", [P, CT, 3 * C], fp16)
        wo = sb("wo", [P, CT, C])
        ind = sb("ind", [P, HW], fp16)
        toep = sb("toep", [P, 2, NM, BAND])
        t_hw = sb("t_hw", [P, 2 * DJ, 2, W])
        t_1d = sb("t_1d", [P, 3, W1D])
        bias = sb("bias", [P, 4, 2, CT, TOK])
        ident = sb("ident", [P, P])
        gavg = sb("gavg", [P, P])
        ones3 = sb("ones3", [3, P], fp16)
        ones256 = sb("ones256", [P, 1])
        zrow = sb("zrow", [1, 2 * P + 2 * PAD])
        uw = sb("uw", [P, W])
        half = sb("half", [P, 2])
        neg_half = sb("neg_half", [P, CT])
        bnp = sb("bnp", [P, 4, 3])
        bn_s = sb("bn_s", [P, 3])
        bn_b = sb("bn_b", [P, 3])
        w1 = sb("w1", [P, CT, HID])
        w2 = sb("w2", [HID, C])
        bq = sb("bq", [P, 6])
        bo = sb("bo", [P, CT])
        bvo = sb("bvo", [P, CT])
        q_scale = sb("q_scale", [P, 2])
        q_bias = sb("q_bias", [P, CT, 2])
        gm = sb("gm", [P, 8])
        conv_inv, qkv_inv = gm[:, 6:7], gm[:, 7:8]

        raw = sb("raw", [P, CT, 4, W])
        Z = sb("Z", [P, CT, 2, 2, PT])
        Z3 = sb("Z3", [P, 2, PAIRS + DJ - 1])
        yt = sb("yt", [W, 2, C])
        s12 = sb("s12", [P, CT, 2, W])
        s3 = sb("s3", [P, PAIRS])
        s3t = sb("s3t", [PAIRS, 3, P], fp16)
        srow = sb("srow", [3, HW], fp16)
        ab = sb("ab", [P, CT, P])
        ab_hi = sb("ab_hi", [P, C], fp16)
        ab_lo = sb("ab_lo", [P, C], fp16)
        w3c = sb("w3c", [P, CT, 3])
        w3h = sb("w3h", [P, CT], fp16)
        w3t = sb("w3t", [3, C], fp16)
        wt = sb("wt", [P, CT, 3])
        sm = sb("sm", [P, 4, CT])
        part = sb("part", [P, CT, NCH])
        pooled = sb("pooled", [P, CT])
        stats = sb("stats", [P, CT, NCH, 6])
        mv = sb("mv", [P, CT, 2])
        gn = sb("gn", [P, 6, CT])
        g_mean, g_dev, g_sq, g_ve, g_r, g_b = (gn[:, i, :] for i in range(6))
        al = sb("al", [P, 2, 5])
        r64 = sb("r64", [P, CT])
        y1 = sb("y1", [P, CT, H])
        ysum = sb("ysum", [P, 2, CT])
        hid = sb("hid", [HID, 1])
        wch = sb("wch", [P, 6, CT])
        alpha, beta, a3, b3, beta_o = (wch[:, i, :] for i in range(1, 6))
        tmp = sb("tmp", [P, 4, CHUNK])
        tok = sb("tok", [P, CT, CHUNK])
        tok_hi = sb("tok_hi", [P, CT, CHUNK], fp16)
        tok_lo = sb("tok_lo", [P, CT, CHUNK], fp16)
        qbd = sb("qbd", [P, CT, NW, 2, TOK])
        kk = sb("kk", [P, CT, CHUNK])
        vv = sb("vv", [P, NW // 2, C])
        sc = sb("sc", [P, 2, CHUNK])
        pr = sb("pr", [P, 2, CHUNK])
        prt = sb("prt", [P, 2, CHUNK])
        mx = sb("mx", [P, 2, 8])
        sums = sb("sums", [P, 2, 8])
        rec = sb("rec", [P, 2, 8])
        ot = sb("ot", [P, CT, CHUNK])

        F = ps("F", [P, 2, CHUNK])
        QP = ps("QP", [P, CHUNK])
        SP = ps("SP", [P, 2, CHUNK])
        PTR = ps("PTR", [P, CHUNK])
        O = ps("O", [P, 2, CHUNK])

        scratch_t = nc.dram_tensor("scratch_t", (P, T_ALL), fp32)
        scratch_w = nc.dram_tensor("scratch_w", (C, C * TAPS), fp32)

        consts_in = sem("consts_in")
        zero_set = sem("zero_set")
        zero_out = sem("zero_out")
        bands_out = sem("bands_out")
        bands_in = sem("bands_in")
        wconv_in = sem("wconv_in")
        wcirc_set = sem("wcirc_set")
        wcirc_out = sem("wcirc_out")
        wrow_in = sem("wrow_in")
        bias_rev_in = sem("bias_rev_in")
        setup_max = sem("setup_max")
        setup_gmax = sem("setup_gmax")
        setup_scaled = sem("setup_scaled")
        setup_tr = sem("setup_tr")
        setup_hi = sem("setup_hi")
        setup_lo = sem("setup_lo")
        setup_exp = sem("setup_exp")
        setup_bn = sem("setup_bn")
        x_loaded = sem("x_loaded")
        dve_seq = sem("dve_seq")
        act_seq = sem("act_seq")
        pool_seq = sem("pool_seq")
        gn_stats = sem("gn_stats")
        gn_mean = sem("gn_mean")
        gn_sq = sem("gn_sq")
        gn_var = sem("gn_var")
        gn_ve = sem("gn_ve")
        gn_rstd = sem("gn_rstd")
        gn_coef = sem("gn_coef")
        g_ready = sem("g_ready")
        f_tr = sem("f_tr")
        f_max = sem("f_max")
        z_ready = sem("z_ready")
        y_done = sem("y_done")
        y_copied = sem("y_copied")
        y_tr = sem("y_tr")
        e12_ready = sem("e12_ready")
        s12_ready = sem("s12_ready")
        csum_done = sem("csum_done")
        z3_ready = sem("z3_ready")
        y3_done = sem("y3_done")
        e3_ready = sem("e3_ready")
        s3_ready = sem("s3_ready")
        s3_tr = sem("s3_tr")
        s3_split = sem("s3_split")
        srow_in = sem("srow_in")
        s3b_done = sem("s3b_done")
        s3b_used = sem("s3b_used")
        pooled_set = sem("pooled_set")
        logits_done = sem("logits_done")
        lg_ready = sem("lg_ready")
        lg_exp = sem("lg_exp")
        ab_set = sem("ab_set")
        ab_tr = sem("ab_tr")
        ab_hi_set = sem("ab_hi_set")
        ab_lo_set = sem("ab_lo_set")
        gate_done = sem("gate_done")
        gated = sem("gated")
        x1_set = sem("x1_set")
        pads_set = sem("pads_set")
        nrm_set = sem("nrm_set")
        hi_set = sem("hi_set")
        lo_set = sem("lo_set")
        conv_done = sem("conv_done")
        x2_set = sem("x2_set")
        dwt_mul = sem("dwt_mul")
        dwt_used = sem("dwt_used")
        se_y = sem("se_y")
        se_h = sem("se_h")
        se_relu = sem("se_relu")
        se_z = sem("se_z")
        se_exp = sem("se_exp")
        coef3 = sem("coef3")
        tok_set = sem("tok_set")
        tok_hi_set = sem("tok_hi_set")
        tok_lo_set = sem("tok_lo_set")
        x3_set = sem("x3_set")
        qp_done = sem("qp_done")
        qp_read = sem("qp_read")
        s_done = sem("s_done")
        s_biased = sem("s_biased")
        s_max = sem("s_max")
        s_sub = sem("s_sub")
        p_exp = sem("p_exp")
        p_rec = sem("p_rec")
        p_norm = sem("p_norm")
        pt_done = sem("pt_done")
        pt_read = sem("pt_read")
        pv_done = sem("pv_done")
        o_read = sem("o_read")
        x4_set = sem("x4_set")
        stored = sem("stored")

        class Chain:

            def __init__(self, eng, s):
                self.eng, self.s, self.n = eng, s, 0

            def link(self, ins):
                self.n += 1
                ins.then_inc(self.s, 1)
                self.eng.wait_ge(self.s, self.n)

        def dram(t, offset, dims):
            return bass.AP(t.tensor if isinstance(t, bass.AP) else t, offset, dims)

        def clear_semaphores():
            with nc.Block() as block:
                @block.gpsimd
                def _(pool):
                    for s in sems:
                        pool.sem_clear(s)

        WB = X[:, :, :].rearrange("p t n -> p (t n)")[:, 0:BMAX * 2 * BMAX * TAPS]
        WR = X[:, :, :].rearrange("p t n -> p (t n)")[:, 0:CT * C * TAPS].rearrange("p (t n) -> p t n", t=CT)
        acc = Gn.rearrange("p t n -> p (t n)")[:, 0:BMAX * 2 * BMAX * TAPS]
        tc = toep[:, :, :, :].rearrange("p a b c -> p (a b c)")[:, 0:BMAX * BMAX * TAPS]
        qkv_f = Gn.rearrange("p t n -> p (t n)")[:, 0:CT * 3 * C].rearrange("p (t n) -> p t n", t=CT)
        tcr = sb("tcr", [P, BMAX * BMAX * TAPS]) if False else Gn.rearrange("p t n -> p (t n)")[:, 4608:4608 + 2304]
        zeros = Gn.rearrange("p t n -> p (t n)")[:, 0:T_ALL]
        bias_rev = tok[:, :, :].rearrange("p t n -> p (t n)")[:, 0:2 * CT * TOK].rearrange(
            "p (s t m) -> p s t m", s=2, t=CT)
        mask = tmp[:, 0, 0:4 * TOK].rearrange("p (y m) -> p y m", y=4)

        with nc.Block() as block:
            small = [(gavg[:, :], c_gavg), (ident[:, :], c_ident), (ind[:, :], c_ind), (ones3[:, :], c_ones3),
                     (half[:, :], c_half), (w2[:, :], w2t),
                     (w1[:, :, :], w1t.rearrange("(t p) n -> p t n", p=P)),
                     (wo[:, :, :], w_o.rearrange("(t p) n -> p t n", p=P)),
                     (bq[:, :], b_qkv),
                     (bo[:, :], b_o),
                     (bnp[:, :, :], dram(bn, 0, [[0, P], [3, 4], [1, 3]])),
                     (al[:, 0, :], dram(alphas, 0, [[0, P], [1, 5]])),
                     (uw[:, :], dram(c_u, 0, [[0, P], [1, W]])),
                     (mask, c_mask)]

            @block.sync
            def _(sp):
                for q in range(C // BMAX):
                    sp.dma_start(WB[8 * q:8 * q + 8, :].rearrange("p (r n) -> p r n", r=BMAX),
                                 dram(w_conv, q * BMAX * C * TAPS,
                                      [[2 * BMAX * TAPS, 8], [C * TAPS, BMAX], [1, 2 * BMAX * TAPS]])
                                 ).then_inc(wconv_in, 16)
                for dst, src in small:
                    sp.dma_start(dst, src).then_inc(consts_in, 16)
                sp.wait_ge(zero_set, 1)
                sp.dma_start(scratch_t[:, :], zeros).then_inc(zero_out, 16)
                sp.wait_ge(zero_out, 16)
                n = 0
                for m, k in enumerate((k_cw, k_hc)):
                    sp.dma_start(dram(scratch_t, T_CW + m * NM * BAND, [[T_ALL + 1, P], [BAND, NM], [1, KS]]),
                                 dram(k, 0, [[0, P], [KS, NM], [1, KS]])).then_inc(bands_out, 16)
                    n += 1
                for a in range(2):
                    for b in range(2):
                        for dj in range(DJ):
                            kh = 2 * (dj - 2) + a - b + PAD
                            if 0 <= kh < KS:
                                sp.dma_start(dram(scratch_t, a * W * T_ALL + T_HW + dj * 2 * PT + b * PT,
                                                  [[T_ALL + 1, W], [DJ * 2 * PT, 2], [1, KS]]),
                                             dram(k_hw, kh * KS, [[0, W], [KS * KS, 2], [1, KS]])
                                             ).then_inc(bands_out, 16)
                                n += 1
                sp.dma_start(dram(scratch_t, T_1D + P - PAD, [[T_ALL + 1, P], [W1D, 3], [1, KS]]),
                             dram(k_1d, 0, [[0, P], [KS, 3], [1, KS]])).then_inc(bands_out, 16)
                n += 1
                sp.wait_ge(bands_out, 16 * n)
                sp.wait_ge(wcirc_set, 1)
                sp.dma_start(toep[:, :, :, :].rearrange("p a b c -> p (a b c)"),
                             scratch_t[:, T_CW:T_HW]).then_inc(bands_in, 16)
                sp.dma_start(t_hw[:, :, :, :],
                             scratch_t[:, T_HW:T_1D].rearrange("p (m a w) -> p m a w", a=2, w=PT)[:, :, :, PAD:PAD + W]
                             ).then_inc(bands_in, 16)
                sp.dma_start(t_1d[:, :, :], scratch_t[:, T_1D:T_ALL].rearrange("p (k n) -> p k n", k=3)
                             ).then_inc(bands_in, 16)
                for q in range(C // BMAX):
                    sp.dma_start(dram(scratch_w, q * BMAX * C * TAPS,
                                      [[2 * BMAX * TAPS, 8], [C * TAPS, BMAX], [1, 2 * BMAX * TAPS]]),
                                 acc[8 * q:8 * q + 8, :].rearrange("p (r n) -> p r n", r=BMAX)
                                 ).then_inc(wcirc_out, 16)
                sp.wait_ge(wcirc_out, 16 * (C // BMAX))
                sp.dma_start(WR, scratch_w[:, :].rearrange("(t p) n -> p t n", p=P)).then_inc(wrow_in, 16)
                sp.dma_start(qkv_f, w_qkv.rearrange("(t p) n -> p t n", p=P)).then_inc(wrow_in, 16)
                sp.wait_ge(bands_in, 48)

            @block.gpsimd
            def _(pool):
                seq = Chain(pool, pool_seq)
                pool.memset(zeros, 0.0).then_inc(zero_set, 1)
                pool.memset(ones256[:, :], 1.0 / C)
                pool.memset(zrow[:, :], 0.0)
                pool.memset(neg_half[:, :], -0.5)
                pool.memset(Z[:, :, :, :, :], 0.0)
                pool.memset(Z3[:, :, :], 0.0)
                n = 0
                for h in range(HEADS):
                    cg, hs, h2 = h // 4, h // 2 % 2, h % 2
                    for yq in range(WS):
                        pool.dma_start(bias_rev[64 * h2 + 8 * yq:64 * h2 + 8 * yq + 8, hs, cg, :]
                                       .rearrange("p (y x) -> p y x", y=WS),
                                       dram(rel_t, h * (2 * WS - 1) ** 2 + yq * (2 * WS - 1),
                                            [[1, WS], [2 * WS - 1, WS], [1, WS]])).then_inc(bias_rev_in, 16)
                pool.wait_ge(consts_in, 16 * len(small))
                seq.link(pool.tensor_scalar(bn_s[:, :], bnp[:, 3, :], EPS, None, ALU.add))
                seq.link(pool.memset(gm[:, 0:3], -0.5))
                seq.link(pool.tensor_tensor(bn_s[:, :], bn_s[:, :], gm[:, 0:3], ALU.pow))
                seq.link(pool.tensor_tensor(bn_s[:, :], bn_s[:, :], bnp[:, 0, :], ALU.mult))
                seq.link(pool.tensor_tensor(bn_b[:, :], bn_s[:, :], bnp[:, 2, :], ALU.mult))
                seq.link(pool.tensor_tensor(bn_b[:, :], bnp[:, 1, :], bn_b[:, :], ALU.subtract))
                pool.tensor_scalar(bn_b[:, :], bn_b[:, :], 0.5, None, ALU.mult)
                pool.tensor_scalar(bn_s[:, :], bn_s[:, :], 0.5, None, ALU.mult).then_inc(setup_bn, 1)
                for i in range(2):
                    pool.wait_ge(setup_max, i + 1)
                    pool.partition_all_reduce(gm[:, 2 + i:3 + i], gm[:, i:i + 1], P, ABSMAX).then_inc(setup_gmax, 1)

            @block.scalar
            def _(act):
                act.wait_ge(setup_exp, 1)
                S.activation(al[:, 0, :], al[:, 1, :], ACT.Exp).then_inc(act_seq, 1)
                for n in range(18):
                    act.wait_ge(setup_tr, n + 1)
                    ti, tap = n // 9, n % 9
                    if True:
                        S.activation(cw_hi[:, ti, tap, :], F[:, n % 2, 0:C], ACT.Copy).then_inc(setup_hi, 1)

            @block.vector
            def _(dve):
                seq = Chain(dve, dve_seq)
                dve.wait_ge(consts_in, 16 * len(small))
                seq.link(V.reduce_max(sm[:, 0, 0:1], al[:, 0, :], AX.X))
                V.tensor_scalar(al[:, 1, :], al[:, 0, :], sm[:, 0, 0:1], None, ALU.subtract).then_inc(setup_exp, 1)
                dve.wait_ge(act_seq, 1)
                seq.link(V.reduce_sum(sm[:, 1, 0:1], al[:, 0, :], AX.X))
                seq.link(V.reciprocal(sm[:, 2, 0:1], sm[:, 1, 0:1]))
                seq.link(V.tensor_scalar(al[:, 1, :], al[:, 0, :], sm[:, 2, 0:1], None, ALU.mult))
                dve.wait_ge(wconv_in, 16 * (C // BMAX))
                dve.wait_ge(zero_out, 16)
                seq.link(V.tensor_scalar(acc, WB, al[:, 1, 0:1], None, ALU.mult))
                for n, b in enumerate(BLOCKS):
                    size = BMAX * 2 * BMAX // b * TAPS
                    rb, pc = BMAX // b, 2 * BMAX // b

                    def blocks(ap, j, lo, count):
                        v = ap.rearrange("p (R r q c) -> p R r q c", R=rb, r=b, q=pc)
                        return v[:, :, j, :, lo * TAPS:(lo + count) * TAPS]

                    def diag(ap, lo, count):
                        v = ap[:, 0:size].rearrange("p (R q c) -> p R q c", R=rb, q=pc)
                        return v[:, :, :, lo * TAPS:(lo + count) * TAPS]

                    seq.link(V.tensor_copy(diag(tc, 0, b), blocks(WB, 0, 0, b)))
                    for j in range(1, b):
                        V.tensor_tensor(diag(tc, 0, b - j), diag(tc, 0, b - j), blocks(WB, j, j, b - j), ALU.add)
                        seq.link(V.tensor_tensor(diag(tc, b - j, j), diag(tc, b - j, j), blocks(WB, j, 0, j), ALU.add))
                    for i in range(b):
                        last = V.tensor_scalar(diag(tcr, i, 1), diag(tc, (-i) % b, 1), al[:, 1, n + 1:n + 2],
                                               1.0 / b, ALU.mult, ALU.mult)
                    seq.link(last)
                    for r in range(b):
                        if r:
                            V.tensor_tensor(blocks(acc, r, 0, r), blocks(acc, r, 0, r), diag(tcr, b - r, r), ALU.add)
                        last = V.tensor_tensor(blocks(acc, r, r, b - r), blocks(acc, r, r, b - r),
                                               diag(tcr, 0, b - r), ALU.add)
                    seq.link(last)
                V.memset(sm[:, 3, :], 0.0).then_inc(wcirc_set, 1)
                dve.wait_ge(bias_rev_in, 16 * HEADS * WS)
                for y in range(4):
                    for hs in range(2):
                        for cg in range(CT):
                            V.tensor_tensor(bias[:, y, hs, cg, :], bias_rev[:, hs, cg, ::-1], mask[:, y, :], ALU.add)
                dve.wait_ge(wrow_in, 32)
                dve.wait_ge(setup_bn, 1)
                V.tensor_reduce(gm[:, 0:1], WR, AX.XY, ALU.max, apply_absolute_value=True).then_inc(setup_max, 1)
                V.tensor_reduce(gm[:, 1:2], qkv_f, AX.XY, ALU.max, apply_absolute_value=True).then_inc(setup_max, 1)
                dve.wait_ge(setup_gmax, 2)
                seq.link(V.tensor_scalar(gm[:, 2:4], gm[:, 2:4], 1e-30, None, ALU.max))
                seq.link(V.reciprocal(gm[:, 4:6], gm[:, 2:4]))
                V.tensor_scalar(gm[:, 6:8], gm[:, 2:4], 1.0 / FULL, None, ALU.mult)
                seq.link(V.tensor_scalar(gm[:, 4:6], gm[:, 4:6], FULL, None, ALU.mult))
                V.tensor_scalar(WR, WR, gm[:, 4:5], None, ALU.mult).then_inc(setup_scaled, 1)
                seq.link(V.tensor_scalar(qkv_f, qkv_f, gm[:, 5:6], None, ALU.mult))
                seq.link(V.tensor_copy(qkv_hi[:, :, :], qkv_f))
                V.tensor_tensor(qkv_lo[:, :, :], qkv_f, qkv_hi[:, :, :], ALU.subtract)
                seq.link(V.tensor_scalar(q_scale[:, :], half[:, :], qkv_inv, DH ** -0.5, ALU.mult, ALU.mult))
                for cg in range(CT):
                    V.tensor_scalar(q_bias[:, cg, :], half[:, :], bq[:, cg:cg + 1], DH ** -0.5, ALU.mult, ALU.mult)
                for n in range(18):
                    ti, tap = n // 9, n % 9
                    dve.wait_ge(setup_hi, n + 1)
                    V.tensor_tensor(cw_lo[:, ti, tap, :], F[:, n % 2, 0:C], cw_hi[:, ti, tap, :],
                                    ALU.subtract).then_inc(setup_lo, 1)
                dve.wait_ge(setup_tr, 19)
                V.tensor_tensor(bvo[:, :], QP[:, 0:CT], bo[:, :], ALU.add)

            @block.tensor
            def _(pe):
                pe.wait_ge(setup_scaled, 1)
                pe.wait_ge(consts_in, 16 * len(small))
                rows = WR.rearrange("p t (i k) -> p t i k", k=TAPS)
                for n in range(18):
                    ti, tap = n // 9, n % 9
                    if n >= 2:
                        pe.wait_ge(setup_lo, n - 1)
                    for to in range(CT):
                        last = T.transpose(F[:, n % 2, P * to:P * to + P], rows[:, to, P * ti:P * ti + P, tap],
                                           ident[:, :])
                    last.then_inc(setup_tr, 1)
                for co in range(CT):
                    for ci in range(CT):
                        last = T.matmul(QP[:, co:co + 1], wo[:, ci, P * co:P * co + P], bq[:, 4 + ci:5 + ci],
                                        start=(ci == 0), stop=(ci == CT - 1))
                last.then_inc(setup_tr, 1)

        def window_pieces(r):
            for i0, i1, row in ([(0, WS, WS * r + SHIFT)] if r < NW - 1 else
                                [(0, SHIFT, WS * r + SHIFT), (SHIFT, WS, 0)]):
                yield 0, NW - 1, i0, i1, 0, WS, row, SHIFT
                yield NW - 1, NW, i0, i1, 0, SHIFT, row, W - SHIFT
                yield NW - 1, NW, i0, i1, SHIFT, WS, row, 0

        def image_piece(t, piece):
            w0, w1_, i0, i1, j0, j1, row, col = piece
            rows = X[:, t, :].rearrange("p (r c) -> p r c", r=H)[:, row:row + i1 - i0, :]
            n = (w1_ - w0) * (j1 - j0)
            return rows[:, :, col:col + n].rearrange("p r (w j) -> p w r j", j=j1 - j0)

        def token_piece(ap, piece):
            w0, w1_, i0, i1, j0, j1, row, col = piece
            return ap.rearrange("p (w i j) -> p w i j", w=NW, i=WS)[:, w0:w1_, i0:i1, j0:j1]

        def rowmajor_piece(ap, piece):
            w0, w1_, i0, i1, j0, j1, row, col = piece
            return ap.rearrange("p (i w j) -> p w i j", w=NW, i=WS)[:, w0:w1_, i0:i1, j0:j1]

        clear_semaphores()
        with nc.Fori(0, NB) as image:
          with nc.Block() as block:
            Zv = Z[:, :, :, :, :]

            @block.sync
            def _(sp):
                for t in range(CT):
                    sp.dma_start(X[:, t, :], x[bass.ds(image, 1), P * t:P * t + P, :].rearrange("b p n -> p (b n)")
                                 ).then_inc(x_loaded, 16)
                sp.wait_ge(s3_split, 1)
                for k in range(3):
                    sp.dma_start(srow[k:k + 1, :].rearrange("k (j p) -> k j p", p=P), s3t[:, k, :]
                                 ).then_inc(srow_in, 16)
                sp.wait_ge(x4_set, NW)
                for t in range(CT):
                    sp.dma_start(out[bass.ds(image, 1), P * t:P * t + P, :].rearrange("b p n -> p (b n)"),
                                 X[:, t, :]).then_inc(stored, 16)
                sp.wait_ge(stored, 16 * CT)

            @block.gpsimd
            def _(pool):
                seq = Chain(pool, pool_seq)

                def rstd(n):
                    pool.wait_ge(gn_ve, n + 1)
                    G.tensor_tensor(g_r, g_ve, neg_half[:, :], ALU.pow).then_inc(gn_rstd, 1)

                rstd(0)
                for n in range(CT * NCH):
                    k, t = divmod(n, CT)
                    pool.wait_ge(gated, n + 1)
                    piece = slice(CHUNK * k, CHUNK * k + CHUNK)
                    G.tensor_tensor(X[:, t, piece], X[:, t, piece], Gn[:, t, piece], ALU.add).then_inc(x1_set, 1)
                pool.wait_ge(x1_set, CT * NCH)
                for l in range(2):
                    for t in range(CT):
                        G.memset(halves[:, l, t, 0::HP - 1, :], 0.0)
                        last = G.memset(halves[:, l, t, 1:HP - 1, 0::HP - 1], 0.0)
                last.then_inc(pads_set, 1)
                rstd(1)
                for n in range(CT * NCH):
                    k, t = divmod(n, CT)
                    pool.wait_ge(nrm_set, n + 1)
                    G.tensor_copy(halves[:, 0, t, 1 + ROWS * k:1 + ROWS * k + ROWS, 1:1 + W],
                                  tmp[:, n % 4, :].rearrange("p (r c) -> p r c", c=W)).then_inc(hi_set, 1)
                for n in range(CT * NCH):
                    k, t = divmod(n, CT)
                    pool.wait_ge(x2_set, n + 1)
                    if n >= 4:
                        pool.wait_ge(dwt_used, n - 3)
                    else:
                        pool.wait_ge(lo_set, CT * NCH)
                    G.tensor_tensor(tmp[:, n % 4, :].rearrange("p (r c) -> p r c", c=W),
                                    X[:, t, CHUNK * k:CHUNK * k + CHUNK].rearrange("p (r c) -> p r c", c=W),
                                    uw[:, :].unsqueeze(1).to_broadcast([P, ROWS, W]), ALU.mult).then_inc(dwt_mul, 1)
                rstd(2)
                rstd(3)
                for r in range(NW):
                    if r:
                        pool.wait_ge(qp_done, 8 * r - 2)
                    for t in range(CT):
                        pool.wait_ge(tok_set, CT * r + t + 1)
                        G.tensor_copy(tok_hi[:, t, :].rearrange("p (w i j) -> p w i j", w=NW, i=WS),
                                      tok[:, t, :].rearrange("p (i w j) -> p w i j", w=NW, i=WS)
                                      ).then_inc(tok_hi_set, 1)
                    for u in range(4 * r, 4 * r + 4):
                        hs = u % 2
                        pool.wait_ge(s_max, u + 1)
                        G.tensor_tensor(sc[:, hs, :].rearrange("p (n m) -> p n m", m=TOK),
                                        sc[:, hs, :].rearrange("p (n m) -> p n m", m=TOK),
                                        mx[:, hs, :].unsqueeze(2).to_broadcast([P, 8, TOK]),
                                        ALU.subtract).then_inc(s_sub, 1)
                        pool.wait_ge(p_rec, u + 1)
                        G.tensor_tensor(pr[:, hs, :].rearrange("p (n m) -> p n m", m=TOK),
                                        pr[:, hs, :].rearrange("p (n m) -> p n m", m=TOK),
                                        rec[:, hs, :].unsqueeze(2).to_broadcast([P, 8, TOK]),
                                        ALU.mult).then_inc(p_norm, 1)

            @block.scalar
            def _(act):
                act.wait_ge(gn_coef, 1)
                for q in range(4):
                    for t in range(CT):
                        piece = slice(HW // 4 * q, HW // 4 * (q + 1))
                        S.activation(Gn[:, t, piece], X[:, t, piece], ACT.Identity, bias=g_b[:, t:t + 1],
                                     scale=g_r[:, t:t + 1]).then_inc(g_ready, 1)
                act.wait_ge(y_done, 2)
                for m in range(2):
                    S.activation(yt[:, m, :], F[0:W, m, PAD:PAD + C], ACT.Copy).then_inc(y_copied, 1)
                act.wait_ge(y_tr, 1)
                for m in range(2):
                    S.activation(s12[:, :, m, :], F[:, 0, 0:4 * W].rearrange("p (t m w) -> p t m w", t=CT, m=2)[:, :, m, :],
                                 ACT.Tanh, bias=bn_b[:, m:m + 1], scale=bn_s[:, m:m + 1]).then_inc(e12_ready, 1)
                act.wait_ge(y3_done, 1)
                S.activation(s3[:, :], F[:, 1, 0:PAIRS], ACT.Tanh, bias=bn_b[:, 2:3],
                             scale=bn_s[:, 2:3]).then_inc(e3_ready, 1)
                act.wait_ge(lg_ready, 1)
                S.activation(wt[:, :, :], wt[:, :, :], ACT.Exp).then_inc(lg_exp, 1)
                act.wait_ge(ab_tr, 1)
                S.activation(ab_hi[:, :], F[:, 0, 0:C], ACT.Copy).then_inc(ab_hi_set, 1)
                S.activation(w3t[:, :], F[0:3, 1, 0:C], ACT.Copy).then_inc(ab_hi_set, 1)
                act.wait_ge(gn_coef, 2)
                act.wait_ge(pads_set, 1)
                for n in range(CT * NCH):
                    k, t = divmod(n, CT)
                    if n >= 4:
                        act.wait_ge(lo_set, n - 3)
                    S.activation(tmp[:, n % 4, :], X[:, t, CHUNK * k:CHUNK * k + CHUNK], ACT.Identity,
                                 bias=g_b[:, t:t + 1], scale=g_r[:, t:t + 1]).then_inc(nrm_set, 1)
                act.wait_ge(se_z, 1)
                S.activation(wch[:, 0, :], F[:, 1, 0:CT], ACT.Tanh, scale=0.5).then_inc(se_exp, 1)
                act.wait_ge(coef3, 1)
                n_qp = 0

                def qp(func):
                    nonlocal n_qp
                    n_qp += 1
                    act.wait_ge(qp_done, n_qp)
                    func().then_inc(qp_read, 1)

                for r in range(NW):
                    for t in range(CT):
                        if r:
                            act.wait_ge(tok_lo_set, CT * r)
                        pieces = list(window_pieces(r))
                        for piece in pieces:
                            last = S.activation(rowmajor_piece(tok[:, t, :], piece), image_piece(t, piece), ACT.Identity,
                                                bias=b3[:, t:t + 1], scale=a3[:, t:t + 1])
                        last.then_inc(tok_set, 1)
                        for piece in pieces:
                            last = S.activation(image_piece(t, piece), image_piece(t, piece), ACT.Identity,
                                                bias=beta_o[:, t:t + 1], scale=alpha[:, t:t + 1])
                        last.then_inc(x3_set, 1)

                    def queries(cg):
                        S.activation(qbd[:, cg, :, 0, :], QP[:, :].rearrange("p (w n) -> p w n", n=TOK), ACT.Identity,
                                     bias=q_bias[:, cg, 0:1], scale=q_scale[:, 0:1])
                        return S.activation(qbd[:, cg, :, 1, :], QP[:, :].rearrange("p (w n) -> p w n", n=TOK),
                                            ACT.Identity, bias=q_bias[:, cg, 1:2], scale=q_scale[:, 1:2])

                    if r:
                        act.wait_ge(s_done, 4 * r)
                    for cg in range(CT):
                        qp(lambda: queries(cg))
                    for cg in range(CT):
                        qp(lambda: S.activation(kk[:, cg, :], QP[:, :], ACT.Identity, bias=bq[:, 2 + cg:3 + cg],
                                                scale=qkv_inv))
                    if r:
                        act.wait_ge(pv_done, 4 * r)
                    for pp in range(2):
                        qp(lambda: S.activation(vv[:, 2 * pp:2 * pp + 2, :].rearrange("p a c -> p (a c)"), QP[:, :],
                                                ACT.Copy, scale=qkv_inv))
                    n_qp += 2
                    for u in range(4 * r, 4 * r + 4):
                        hs = u % 2
                        act.wait_ge(s_sub, u + 1)
                        if u >= 2:
                            act.wait_ge(pt_done, u - 1)
                        S.activation(pr[:, hs, :], sc[:, hs, :], ACT.Exp).then_inc(p_exp, 1)
                        act.wait_ge(pt_done, u + 1)
                        if u >= 2:
                            act.wait_ge(pv_done, u - 1)
                        S.activation(prt[:, hs, :], PTR[:, :], ACT.Copy).then_inc(pt_read, 1)
                    act.wait_ge(pv_done, 4 * r + 4)
                    if r:
                        act.wait_ge(qp_done, 8 * r)
                    for par in range(2):
                        last = S.activation(ot[:, :, :].rearrange("p g (c w n) -> p g c w n", w=2, n=TOK)[:, :, :, par, :],
                                            O[:, par, :].rearrange("p (g c n) -> p g c n", g=CT, n=TOK), ACT.Copy)
                    last.then_inc(o_read, 1)

            @block.vector
            def _(dve):
                seq = Chain(dve, dve_seq)

                def group_norm(n):
                    dve.wait_ge(gn_mean, n + 1)
                    seq.link(V.tensor_copy(g_mean, F[:, 0, 0:CT]))
                    seq.link(V.tensor_tensor(g_dev, mv[:, :, 0], g_mean, ALU.subtract))
                    seq.link(V.tensor_tensor(g_sq, g_dev, g_dev, ALU.mult))
                    V.tensor_tensor(g_sq, g_sq, mv[:, :, 1], ALU.add).then_inc(gn_sq, 1)
                    dve.wait_ge(gn_var, n + 1)
                    V.tensor_scalar(g_ve, F[:, 1, 0:CT], EPS, None, ALU.add).then_inc(gn_ve, 1)
                    dve.wait_ge(gn_rstd, n + 1)
                    V.scalar_tensor_tensor(g_b, g_mean, -1.0, g_r, ALU.mult, ALU.mult).then_inc(gn_coef, 1)
                    dve.wait_ge(gn_coef, n + 1)

                def chunk_stats(n):
                    k, t = divmod(n, CT)
                    return V.bn_stats(stats[:, t, k, :], X[:, t, CHUNK * k:CHUNK * k + CHUNK])

                def moments():
                    for t in range(CT):
                        last = V.bn_aggr(mv[:, t, :], stats[:, t, :, :].rearrange("p k s -> p (k s)"))
                    return last

                dve.wait_ge(x_loaded, 16 * CT)
                for n in range(CT * NCH):
                    last = chunk_stats(n)
                seq.link(last)
                moments().then_inc(gn_stats, 1)
                group_norm(0)
                for t in range(CT):
                    by_col = X[:, t, :].rearrange("p (h w) -> p w h", w=W)
                    by_row = X[:, t, :].rearrange("p (h w) -> p h w", w=W)
                    V.tensor_reduce(raw[:, t, 0, :], by_col, AX.X, ALU.max)
                    V.tensor_reduce(raw[:, t, 1, :], by_col, AX.X, ALU.add)
                    V.tensor_reduce(raw[:, t, 2, :], by_row, AX.X, ALU.max)
                    last = V.tensor_reduce(raw[:, t, 3, :], by_row, AX.X, ALU.add)
                seq.link(last)
                seq.link(V.tensor_scalar(r64[:, :], g_r, 1.0 / W, None, ALU.mult))
                for t in range(CT):
                    V.tensor_scalar(Zv[:, t, :, 0, PAD:PAD + W], raw[:, t, 0::2, :], g_r[:, t:t + 1], g_b[:, t:t + 1],
                                    ALU.mult, ALU.add)
                    last = V.tensor_scalar(Zv[:, t, :, 1, PAD:PAD + W], raw[:, t, 1::2, :], r64[:, t:t + 1],
                                           g_b[:, t:t + 1], ALU.mult, ALU.add)
                last.then_inc(z_ready, 1)
                for jj in range(PAIRS // 2):
                    dve.wait_ge(f_tr, jj + 1)
                    V.tensor_reduce(Z3[:, 0, 2 + 2 * jj:4 + 2 * jj], F[:, jj % 2, :].rearrange("p (j c) -> p j c", j=2),
                                    AX.X, ALU.max).then_inc(f_max, 1)
                dve.wait_ge(e12_ready, 2)
                V.tensor_scalar(s12[:, :, :, :], s12[:, :, :, :], 0.5, 0.5, ALU.mult, ALU.add).then_inc(s12_ready, 1)
                dve.wait_ge(csum_done, 1)
                V.tensor_copy(Z3[:, 1, 2:2 + PAIRS], F[:, 0, 0:PAIRS]).then_inc(z3_ready, 1)
                dve.wait_ge(e3_ready, 1)
                V.tensor_scalar(s3[:, :], s3[:, :], 0.5, 0.5, ALU.mult, ALU.add).then_inc(s3_ready, 1)
                dve.wait_ge(s3_tr, 1)
                seq.link(V.tensor_copy(s3t[:, 0, :], F[0:PAIRS, 0, 0:P]))
                V.tensor_copy(s3t[:, 2, :], s3t[:, 0, :])
                V.tensor_tensor(s3t[:, 1, :], F[0:PAIRS, 0, 0:P], s3t[:, 0, :], ALU.subtract).then_inc(s3_split, 1)
                dve.wait_ge(s12_ready, 1)
                for t in range(CT):
                    last = V.tensor_tensor_reduce(out=tmp[:, t, 0:2 * W].rearrange("p (m w) -> p m w", m=2), in0=s12[:, t, :, :],
                                           in1=Zv[:, t, :, 1, PAD:PAD + W], scale=1.0, scalar=0.0,
                                           op0=ALU.mult, op1=ALU.add, accum_out=sm[:, 0, t:t + 1])
                seq.link(last)
                for k in range(NCH):
                    dve.wait_ge(s3b_done, k + 1)
                    if k >= 2:
                        dve.wait_ge(s3b_used, k - 1)
                    for t in range(CT):
                        last = V.tensor_tensor_reduce(out=tmp[:, 2 * (k % 2) + t, :], in0=F[:, k % 2, :],
                                                      in1=Gn[:, t, CHUNK * k:CHUNK * k + CHUNK], scale=1.0, scalar=0.0,
                                                      op0=ALU.mult, op1=ALU.add, accum_out=part[:, t, k:k + 1])
                    last.then_inc(s3b_used, 1)
                dve.wait_ge(s3b_used, NCH)
                seq.link(V.reduce_sum(sm[:, 1, :], part[:, :, :], AX.X))
                seq.link(V.tensor_scalar(sm[:, 1, :], sm[:, 1, :], 1.0 / (3 * HW), None, ALU.mult))
                V.scalar_tensor_tensor(pooled[:, :], sm[:, 0, :], 1.0 / (3 * W), sm[:, 1, :],
                                       ALU.mult, ALU.add).then_inc(pooled_set, 1)
                dve.wait_ge(logits_done, 1)
                logits = F[:, 0, 0:3 * CT].rearrange("p (t k) -> p t k", k=3)
                seq.link(V.reduce_max(sm[:, 2, :], logits, AX.X))
                V.tensor_tensor(wt[:, :, :], logits, sm[:, 2, :].unsqueeze(2).to_broadcast([P, CT, 3]),
                                ALU.subtract).then_inc(lg_ready, 1)
                dve.wait_ge(lg_exp, 1)
                seq.link(V.reduce_sum(sm[:, 0, :], wt[:, :, :], AX.X))
                seq.link(V.reciprocal(sm[:, 1, :], sm[:, 0, :]))
                seq.link(V.tensor_tensor(wt[:, :, :], wt[:, :, :], sm[:, 1, :].unsqueeze(2).to_broadcast([P, CT, 3]),
                                         ALU.mult))
                for t in range(CT):
                    for m in range(2):
                        V.tensor_scalar(ab[:, t, W * m:W * m + W], s12[:, t, m, :], wt[:, t, m:m + 1], None, ALU.mult)
                seq.link(V.tensor_copy(w3h[:, :], wt[:, :, 2]))
                V.tensor_copy(w3c[:, :, 0], w3h[:, :])
                V.tensor_copy(w3c[:, :, 1], w3h[:, :])
                V.tensor_tensor(w3c[:, :, 2], wt[:, :, 2], w3h[:, :], ALU.subtract).then_inc(ab_set, 1)
                dve.wait_ge(ab_hi_set, 2)
                V.tensor_tensor(ab_lo[:, :], F[:, 0, 0:C], ab_hi[:, :], ALU.subtract).then_inc(ab_lo_set, 1)
                for n in range(CT * NCH + 2):
                    if n < CT * NCH:
                        k, t = divmod(n, CT)
                        dve.wait_ge(gate_done, n + 1)
                        V.tensor_tensor(Gn[:, t, CHUNK * k:CHUNK * k + CHUNK], Gn[:, t, CHUNK * k:CHUNK * k + CHUNK],
                                        F[:, n % 2, :], ALU.mult).then_inc(gated, 1)
                    if n >= 2:
                        dve.wait_ge(x1_set, n - 1)
                        last = chunk_stats(n - 2)
                seq.link(last)
                moments().then_inc(gn_stats, 1)
                group_norm(1)
                for n in range(CT * NCH):
                    k, t = divmod(n, CT)
                    dve.wait_ge(hi_set, n + 1)
                    rows = slice(1 + ROWS * k, 1 + ROWS * k + ROWS)
                    V.tensor_tensor(halves[:, 1, t, rows, 1:1 + W], tmp[:, n % 4, :].rearrange("p (r c) -> p r c", c=W),
                                    halves[:, 0, t, rows, 1:1 + W], ALU.subtract).then_inc(lo_set, 1)
                for n in range(CT * NCH):
                    k, t = divmod(n, CT)
                    dve.wait_ge(conv_done, n + 1)
                    piece = X[:, t, CHUNK * k:CHUNK * k + CHUNK]
                    V.scalar_tensor_tensor(piece, F[:, n % 2, :], conv_inv, piece, ALU.mult, ALU.add).then_inc(x2_set, 1)
                    dve.wait_ge(x2_set, n + 1)
                    last = chunk_stats(n)
                    dve.wait_ge(dwt_mul, n + 1)
                    V.tensor_reduce(y1[:, t, ROWS * k:ROWS * k + ROWS], tmp[:, n % 4, :].rearrange("p (r c) -> p r c", c=W),
                                    AX.X, ALU.add).then_inc(dwt_used, 1)
                seq.link(last)
                moments().then_inc(gn_stats, 1)
                dve.wait_ge(dwt_used, CT * NCH)
                for t in range(CT):
                    last = V.tensor_tensor_reduce(out=tmp[:, t, 0:H], in0=y1[:, t, :], in1=uw[:, :], scale=1.0, scalar=0.0,
                                                  op0=ALU.mult, op1=ALU.add, accum_out=ysum[:, 0, t:t + 1])
                seq.link(last)
                group_norm(2)
                seq.link(V.tensor_tensor(ysum[:, 0, :], ysum[:, 0, :], g_r, ALU.mult))
                V.scalar_tensor_tensor(ysum[:, 1, :], g_b, u_sum * u_sum, ysum[:, 0, :],
                                       ALU.mult, ALU.add).then_inc(se_y, 1)
                dve.wait_ge(se_h, 1)
                V.tensor_scalar(hid[:, :], F[0:HID, 0, 0:1], 0.0, None, ALU.max).then_inc(se_relu, 1)
                dve.wait_ge(se_exp, 1)
                seq.link(V.tensor_scalar(wch[:, 0, :], wch[:, 0, :], 0.5, 0.5, ALU.mult, ALU.add))
                V.tensor_tensor(beta, wch[:, 0, :], g_b, ALU.mult)
                seq.link(V.tensor_tensor(alpha, wch[:, 0, :], g_r, ALU.mult))
                seq.link(V.tensor_scalar(alpha, alpha, 1.0, None, ALU.add))
                seq.link(V.tensor_tensor(mv[:, :, 0], mv[:, :, 0], alpha, ALU.mult))
                V.tensor_tensor(mv[:, :, 0], mv[:, :, 0], beta, ALU.add)
                seq.link(V.tensor_tensor(mv[:, :, 1], mv[:, :, 1], alpha, ALU.mult))
                V.tensor_tensor(mv[:, :, 1], mv[:, :, 1], alpha, ALU.mult).then_inc(gn_stats, 1)
                dve.wait_ge(gn_stats, 4)
                group_norm(3)
                V.tensor_tensor(a3, alpha, g_r, ALU.mult)
                seq.link(V.tensor_tensor(b3, beta, g_r, ALU.mult))
                V.tensor_tensor(b3, b3, g_b, ALU.add)
                V.tensor_tensor(beta_o, beta, bvo[:, :], ALU.add).then_inc(coef3, 1)

                for r in range(NW):
                    if r:
                        dve.wait_ge(qp_done, 8 * r - 2)
                    for t in range(CT):
                        dve.wait_ge(tok_hi_set, CT * r + t + 1)
                        V.tensor_tensor(tok_lo[:, t, :].rearrange("p (w i j) -> p w i j", w=NW, i=WS),
                                        tok[:, t, :].rearrange("p (i w j) -> p w i j", w=NW, i=WS),
                                        tok_hi[:, t, :].rearrange("p (w i j) -> p w i j", w=NW, i=WS),
                                        ALU.subtract).then_inc(tok_lo_set, 1)
                    for u in range(4 * r, 4 * r + 4):
                        quad, hs = u // 2 % 2, u % 2
                        dve.wait_ge(s_done, u + 1)
                        if u >= 2:
                            dve.wait_ge(p_exp, u - 1)
                        low = 2 * (r == NW - 1)

                        def add_bias(w0, w1_, kind):
                            span = slice(w0, w1_)
                            return V.tensor_tensor(
                                sc[:, hs, :].rearrange("p (g w m) -> p g w m", g=CT, w=4)[:, :, span, :],
                                SP[:, hs, :].rearrange("p (g w m) -> p g w m", g=CT, w=4)[:, :, span, :],
                                bias[:, kind, hs, :, :].unsqueeze(2).to_broadcast([P, CT, w1_ - w0, TOK]), ALU.add)

                        if quad == 0:
                            add_bias(0, 4, low).then_inc(s_biased, 1)
                        else:
                            add_bias(0, 3, low)
                            add_bias(3, 4, low + 1).then_inc(s_biased, 1)
                        dve.wait_ge(s_biased, u + 1)
                        V.tensor_reduce(mx[:, hs, :], sc[:, hs, :].rearrange("p (n m) -> p n m", m=TOK), AX.X,
                                        ALU.max).then_inc(s_max, 1)
                        dve.wait_ge(p_exp, u + 1)
                        seq.link(V.tensor_reduce(sums[:, hs, :], pr[:, hs, :].rearrange("p (n m) -> p n m", m=TOK), AX.X,
                                                 ALU.add))
                        V.reciprocal(rec[:, hs, :], sums[:, hs, :]).then_inc(p_rec, 1)
                    for co in range(CT):
                        dve.wait_ge(qp_done, 8 * r + 7 + co)
                        for piece in window_pieces(r):
                            last = V.tensor_tensor(image_piece(co, piece), image_piece(co, piece),
                                                   token_piece(QP[:, :], piece), ALU.add)
                        last.then_inc(qp_read, 1)
                    V.memset(sm[:, 3, :], 0.0).then_inc(x4_set, 1)

            @block.tensor
            def _(pe):
                def group_norm(n):
                    pe.wait_ge(gn_stats, n + 1)
                    T.matmul(F[:, 0, 0:CT], gavg[:, :], mv[:, :, 0], start=True, stop=True).then_inc(gn_mean, 1)
                    pe.wait_ge(gn_sq, n + 1)
                    T.matmul(F[:, 1, 0:CT], gavg[:, :], g_sq, start=True, stop=True).then_inc(gn_var, 1)

                group_norm(0)
                for jj in range(PAIRS // 2):
                    if jj % (PAIRS // 8) == 0:
                        pe.wait_ge(g_ready, CT * (jj // (PAIRS // 8) + 1))
                    if jj >= 2:
                        pe.wait_ge(f_max, jj - 1)
                    for j in (2 * jj, 2 * jj + 1):
                        for t in range(CT):
                            last = T.transpose(F[:, jj % 2, C * (j % 2) + P * t:C * (j % 2) + P * t + P],
                                               Gn[:, t, P * j:P * j + P], ident[:, :])
                    last.then_inc(f_tr, 1)
                pe.wait_ge(z_ready, 1)
                pe.wait_ge(f_max, PAIRS // 2)
                for m in range(2):
                    T.matmul(F[0:W, m, 0:C + 2 * PAD], zrow[:, 0:W], zrow[:, :], start=True, stop=False,
                             skip_group_check=True)
                    for t in range(CT):
                        for i in range(NM):
                            last = T.matmul(F[0:W, m, P * t:P * t + BAND], Zv[:, t, m, i // KS, i % KS:i % KS + W],
                                            toep[:, m, i, :], start=False, stop=(t == CT - 1 and i == NM - 1),
                                            skip_group_check=True)
                    last.then_inc(y_done, 1)
                pe.wait_ge(y_copied, 2)
                for t in range(CT):
                    for m in range(2):
                        last = T.transpose(F[:, 0, W * (2 * t + m):W * (2 * t + m) + W], yt[:, m, P * t:P * t + P],
                                           ident[0:W, 0:W])
                last.then_inc(y_tr, 1)
                pe.wait_ge(e12_ready, 2)
                for j in range(PAIRS):
                    for t in range(CT):
                        last = T.matmul(F[:, 0, j:j + 1], Gn[:, t, P * j:P * j + P], ones256[:, :],
                                        start=(t == 0), stop=(t == CT - 1))
                last.then_inc(csum_done, 1)
                pe.wait_ge(z3_ready, 1)
                for i in range(2 * DJ):
                    ch, dj = divmod(i, DJ)
                    last = T.matmul(F[:, 1, 0:PAIRS], t_hw[:, i, :, :].rearrange("p a w -> p (a w)"),
                                    Z3[:, ch, dj:dj + PAIRS], start=(i == 0), stop=(i == 2 * DJ - 1))
                last.then_inc(y3_done, 1)
                pe.wait_ge(s3_ready, 1)
                T.transpose(F[0:PAIRS, 0, 0:P], s3[:, :], ident[:, :]).then_inc(s3_tr, 1)
                pe.wait_ge(srow_in, 48)
                pe.wait_ge(s3_split, 1)
                for k in range(NCH):
                    if k >= 2:
                        pe.wait_ge(s3b_used, k - 1)
                    T.matmul(F[:, k % 2, :], ones3[:, :], srow[:, CHUNK * k:CHUNK * k + CHUNK], start=True,
                             stop=True).then_inc(s3b_done, 1)
                pe.wait_ge(pooled_set, 1)
                for to in range(CT):
                    for k in range(3):
                        for ti in range(CT):
                            lo = P * (to - ti + 1)
                            last = T.matmul(F[:, 0, 3 * to + k:3 * to + k + 1], t_1d[:, k, lo:lo + P],
                                            pooled[:, ti:ti + 1], start=(ti == 0), stop=(ti == CT - 1))
                last.then_inc(logits_done, 1)
                pe.wait_ge(ab_set, 1)
                for t in range(CT):
                    T.transpose(F[:, 0, P * t:P * t + P], ab[:, t, :], ident[:, :])
                    last = T.transpose(F[0:3, 1, P * t:P * t + P], w3c[:, t, :], ident[:, :])
                last.then_inc(ab_tr, 1)
                pe.wait_ge(ab_hi_set, 2)
                pe.wait_ge(ab_lo_set, 1)
                for n in range(CT * NCH):
                    k, t = divmod(n, CT)
                    if n >= 2:
                        pe.wait_ge(gated, n - 1)
                    px = slice(CHUNK * k, CHUNK * k + CHUNK)
                    T.matmul(F[:, n % 2, :], ab_hi[:, P * t:P * t + P], ind[:, px], start=True, stop=False)
                    T.matmul(F[:, n % 2, :], ab_lo[:, P * t:P * t + P], ind[:, px], start=False, stop=False)
                    T.matmul(F[:, n % 2, :], w3t[:, P * t:P * t + P], srow[:, px], start=False,
                             stop=True).then_inc(gate_done, 1)
                group_norm(1)
                for n in range(CT * NCH):
                    k, co = divmod(n, CT)
                    if co == 0:
                        pe.wait_ge(lo_set, CT * min(k + 2, NCH))
                    if n >= 2:
                        pe.wait_ge(x2_set, n - 1)
                    first = True
                    for ci in range(CT):
                        for tap in range(TAPS):
                            dy, dx = divmod(tap, C3)
                            win = [halves[:, l, ci, ROWS * k + dy:ROWS * k + dy + ROWS, dx:dx + W] for l in range(2)]
                            for wgt, act_half in ((cw_hi, 0), (cw_hi, 1), (cw_lo, 0)):
                                end = ci == CT - 1 and tap == TAPS - 1 and wgt is cw_lo
                                last = T.matmul(F[:, n % 2, :], wgt[:, ci, tap, P * co:P * co + P], win[act_half],
                                                start=first, stop=end)
                                first = False
                    last.then_inc(conv_done, 1)
                pe.wait_ge(x2_set, CT * NCH)
                group_norm(2)
                pe.wait_ge(se_y, 1)
                for t in range(CT):
                    last = T.matmul(F[0:HID, 0, 0:1], w1[:, t, :], ysum[:, 1, t:t + 1], start=(t == 0), stop=(t == CT - 1))
                last.then_inc(se_h, 1)
                pe.wait_ge(se_relu, 1)
                for t in range(CT):
                    last = T.matmul(F[:, 1, t:t + 1], w2[:, P * t:P * t + P], hid[:, :], start=True, stop=True)
                last.then_inc(se_z, 1)
                group_norm(3)
                n_qp = 0

                def qp_free():
                    if n_qp:
                        pe.wait_ge(qp_read, n_qp)

                HALVES = ((qkv_hi, tok_hi), (qkv_hi, tok_lo), (qkv_lo, tok_hi))
                for r in range(NW):
                    pe.wait_ge(tok_lo_set, CT * (r + 1))
                    pe.wait_ge(tok_hi_set, CT * (r + 1))
                    for oc in range(4):
                        qp_free()
                        for i in range(6):
                            ci, (wgt, tk) = i // 3, HALVES[i % 3]
                            last = T.matmul(QP[:, :], wgt[:, ci, P * oc:P * oc + P], tk[:, ci, :],
                                            start=(i == 0), stop=(i == 5))
                        last.then_inc(qp_done, 1)
                        n_qp += 1
                    for pp in range(2):
                        qp_free()
                        for b in range(2):
                            lo = P * (2 * pp + b)
                            for i in range(6):
                                ci, (wgt, tk) = i // 3, HALVES[i % 3]
                                last = T.matmul(QP[:, C * b:C * b + C], tk[:, ci, lo:lo + P], wgt[:, ci, 2 * C:3 * C],
                                                start=(i == 0), stop=(i == 5))
                        last.then_inc(qp_done, 1)
                        n_qp += 1
                    qp_free()
                    if r:
                        pe.wait_ge(o_read, r)

                    def scores(u):
                        quad, hs = u // 2 % 2, u % 2
                        if u >= 2:
                            pe.wait_ge(s_biased, u - 1)
                        rows = slice(64 * hs, 64 * hs + 64)
                        for cg in range(CT):
                            for w in range(4):
                                win = 4 * quad + w
                                last = T.matmul(SP[:, hs, 256 * cg + TOK * w:256 * cg + TOK * w + TOK],
                                                qbd[rows, cg, win, :, :].rearrange("p h n -> p (h n)"),
                                                kk[rows, cg, TOK * win:TOK * win + TOK], start=True, stop=True)
                        last.then_inc(s_done, 1)

                    def turn(u):
                        hs = u % 2
                        pe.wait_ge(p_norm, u + 1)
                        if u:
                            pe.wait_ge(pt_read, u)
                        for b in range(4):
                            last = T.transpose(PTR[:, P * b:P * b + P], pr[:, hs, P * b:P * b + P], ident[:, :])
                        last.then_inc(pt_done, 1)

                    def weigh(u):
                        quad, hs = u // 2 % 2, u % 2
                        pe.wait_ge(pt_read, u + 1)
                        for b in range(4):
                            cg, wp = divmod(b, 2)
                            pair = 2 * quad + wp
                            for h2 in range(2):
                                h = 4 * cg + 2 * hs + h2
                                for par in range(2):
                                    rows = slice(64 * par, 64 * par + 64)
                                    cols = 256 * cg + TOK * pair
                                    last = T.matmul(O[DH * (h % 4):DH * (h % 4) + DH, par, cols:cols + TOK],
                                                    vv[rows, pair, DH * h:DH * h + DH],
                                                    prt[rows, hs, P * b + TOK * h2:P * b + TOK * h2 + TOK],
                                                    start=True, stop=True)
                        last.then_inc(pv_done, 1)

                    scores(4 * r)
                    scores(4 * r + 1)
                    for u in range(4 * r, 4 * r + 4):
                        turn(u)
                        if u + 2 < 4 * r + 4:
                            scores(u + 2)
                        weigh(u)
                    pe.wait_ge(o_read, r + 1)
                    for co in range(CT):
                        qp_free()
                        for ci in range(CT):
                            last = T.matmul(QP[:, :], wo[:, ci, P * co:P * co + P], ot[:, ci, :],
                                            start=(ci == 0), stop=(ci == CT - 1))
                        last.then_inc(qp_done, 1)
                        n_qp += 1

          clear_semaphores()


def shift_mask():
    img = np.zeros((H, W), np.int32)
    cnt = 0
    for hs in (slice(0, -WS), slice(-WS, -SHIFT), slice(-SHIFT, None)):
        for ws_ in (slice(0, -WS), slice(-WS, -SHIFT), slice(-SHIFT, None)):
            img[hs, ws_] = cnt
            cnt += 1
    mw = img.reshape(NW, WS, NW, WS).transpose(0, 2, 1, 3).reshape(NW, NW, TOK)
    kinds = np.stack([mw[0, 0], mw[0, -1], mw[-1, 0], mw[-1, -1]])
    mask = np.where(kinds[:, :, None] != kinds[:, None, :], -100.0, 0.0).astype(np.float32)
    return np.concatenate([mask.transpose(1, 0, 2)] * 2, axis=0)


def constants():
    gavg = np.kron(np.eye(P // GROUP), np.ones((GROUP, GROUP)) / GROUP).astype(np.float32)
    ind = np.zeros((P, H, W), np.float16)
    ind[np.arange(W), :, np.arange(W)] = 1
    ind[W + np.arange(H), np.arange(H), :] = 1
    ones3 = np.zeros((3, P), np.float16)
    ones3[0:2] = 1
    half = np.zeros((P, 2), np.float32)
    half[np.arange(P), np.arange(P) // DH % 2] = 1
    return {"c_gavg": gavg, "c_ident": np.eye(P, dtype=np.float32), "c_ind": ind.reshape(P, HW),
            "c_ones3": ones3, "c_mask": shift_mask(), "c_u": dwt_mean_weights(W).astype(np.float32), "c_half": half}


def kernel(**inputs):
    import concourse.bacc as _bacc
    from concourse.bass_utils import run_bass_kernel_spmd as _run

    a = {k: np.asarray(v) for k, v in inputs.items()}
    names = ("cw", "hc", "hw")
    bn = np.stack([np.concatenate([a[f"L0_conv_{q}_{n}"] for n in names]) for q in "gbmv"])
    arrays = {
        "x": a["x"].reshape(NB, C, HW),
        "k_cw": a["L0_conv_w_cw"][0].transpose(0, 2, 1)[:, :, ::-1],
        "k_hc": a["L0_conv_w_hc"][0][:, :, ::-1],
        "k_hw": a["L0_conv_w_hw"][0][:, :, ::-1],
        "bn": bn,
        "k_1d": a["L0_conv_w1d"][:, 0, ::-1],
        "w_conv": a["L1_conv_weight"].reshape(C, C * TAPS),
        "alphas": a["L1_conv_alphas"],
        "w1t": a["L2_conv_W1"].T,
        "w2t": a["L2_conv_W2"].T,
        "w_qkv": a["L3_conv_w_qkv"],
        "b_qkv": a["L3_conv_b_qkv"].reshape(-1, P).T,
        "w_o": a["L3_conv_w_o"],
        "b_o": a["L3_conv_b_o"].reshape(-1, P).T,
        "rel_t": a["L3_conv_rel_bias_table"].T,
        **constants(),
    }
    nc = _bacc.Bacc("TRN2", target_bir_lowering=False, num_devices=1)
    feed, args = {}, []
    for name, v in arrays.items():
        v = np.ascontiguousarray(v)
        feed[f"in_{name}"] = v
        args.append(nc.dram_tensor(f"in_{name}", v.shape, mybir.dt.from_np(v.dtype), kind="ExternalInput").ap())
    out = nc.dram_tensor("out_x", (NB, C, HW), mybir.dt.float32, kind="ExternalOutput").ap()
    build(nc, *args, out)
    r = _run(nc, [feed], core_ids=[0])
    return r.results[0]["out_x"].reshape(NB, C, H, W)
```

```python
import numpy as np

import concourse.bass as bass
from concourse import mybir
from contextlib import ExitStack

NB, C, H, W = 8, 256, 64, 64
P = 128
CT = C // P
HW = H * W
CHUNK = 512
NCH = HW // CHUNK
ROWS = CHUNK // W
KS = 7
PAD = KS // 2
BAND = P + 2 * PAD
NM = 2 * KS
PT = W + 2 * PAD
PAIRS = HW // P
DJ = 5
C3 = 3
TAPS = C3 * C3
HP = H + 2
BLOCKS = (2, 4, 8, 16)
BMAX = BLOCKS[-1]
HEADS, WS, SHIFT = 8, 8, 4
DH = C // HEADS
TOK = WS * WS
NW = W // WS
GROUP = 8
HID = C // 16
EPS = 1e-5
FULL = 256.0
T_CW, T_HW, T_1D = 0, 2 * NM * BAND, 2 * NM * BAND + 2 * DJ * 2 * PT
W1D = 3 * P
T_ALL = T_1D + 3 * W1D

DB8_LO = [-0.00011747678400228192, 0.0006754494059985568, -0.0003917403729959771, -0.00487035299301066,
          0.008746094047015655, 0.013981027917015516, -0.04408825393106472, -0.01736930100202211,
          0.128747426620186, 0.00047248457399797254, -0.2840155429624281, -0.015829105256023893,
          0.5853546836548691, 0.6756307362980128, 0.3128715909144659, 0.05441584224308161]


SUM_OPS = 7
SUM_STEPS = [f"stats{i}" for i in range(4)] + [f"reduce{i}" for i in range(8)]
W_L0, W_RED, W_CONV, W_NORM = 1.0, 1.75, 0.5, 1.0


def dwt_mean_weights(n):
    taps = np.asarray(DB8_LO, np.float32).astype(np.float64)
    flen = len(taps)
    source = np.pad(np.arange(n), flen - 1, mode="symmetric")[1:]
    count = (n + flen - 1) // 2
    u = np.zeros(n)
    for m in range(count):
        for k in range(flen):
            u[source[2 * m + k]] += taps[flen - 1 - k] / count
    return u


def build(nc, x, k_cw, k_hc, k_hw, bn, k_1d, w_conv, alphas, w1t, w2t, w_qkv, b_qkv, w_o, b_o,
          rel_t, c_gavg, c_ident, c_ind, c_ones3, c_mask, c_u, c_half, out):
    fp32, fp16 = mybir.dt.float32, mybir.dt.float16
    ALU, ACT, AX = mybir.AluOpType, mybir.ActivationFunctionType, mybir.AxisListType
    ABSMAX = bass.bass_isa.ReduceOp.absmax
    u_sum = float(dwt_mean_weights(W).sum())
    V, S, T, G = nc.vector, nc.scalar, nc.tensor, nc.gpsimd
    ctx = ExitStack()
    with ctx:
        def sb(name, shape, dt=fp32):
            return ctx.enter_context(nc.sbuf_tensor(name, shape, dt))

        def ps(name, shape):
            return ctx.enter_context(nc.psum_tensor(name, shape, fp32))

        def sem(name):
            s = ctx.enter_context(nc.semaphore(name))
            sems.append(s)
            return s

        sems = []
        X = sb("X", [P, CT, HW])
        g_raw = sb("g_raw", [P, CT * 2 * HP * HP], fp16)
        Gn = g_raw[:, 0:CT * HW * 2].bitcast(fp32).rearrange("p (t n) -> p t n", t=CT)
        halves = g_raw[:, :].rearrange("p (l t r c) -> p l t r c", l=2, t=CT, r=HP)
        cw_hi = sb("cw_hi", [P, CT, TAPS, C], fp16)
        cw_lo = sb("cw_lo", [P, CT, TAPS, C], fp16)
        qkv_hi = sb("qkv_hi", [P, CT, 3 * C], fp16)
        qkv_lo = sb("qkv_lo", [P, CT, 3 * C], fp16)
        wo = sb("wo", [P, CT, C])
        ind = sb("ind", [P, HW], fp16)
        toep = sb("toep", [P, 2, NM, BAND])
        t_hw = sb("t_hw", [P, 2 * DJ, 2, W])
        t_1d = sb("t_1d", [P, 3, W1D])
        bias = sb("bias", [P, 4, 2, CT, TOK])
        ident = sb("ident", [P, P])
        gavg = sb("gavg", [P, P])
        ones3 = sb("ones3", [3, P], fp16)
        zrow = sb("zrow", [1, 2 * P + 2 * PAD])
        uw = sb("uw", [P, W])
        half = sb("half", [P, 2])
        neg_half = sb("neg_half", [P, CT])
        bnp = sb("bnp", [P, 4, 3])
        bn_s = sb("bn_s", [P, 3])
        bn_b = sb("bn_b", [P, 3])
        w1 = sb("w1", [P, CT, HID])
        w2 = sb("w2", [HID, C])
        bq = sb("bq", [P, 6])
        bo = sb("bo", [P, CT])
        bvo = sb("bvo", [P, CT])
        q_scale = sb("q_scale", [P, 2])
        q_bias = sb("q_bias", [P, CT, 2])
        gm = sb("gm", [P, 8])
        conv_inv, qkv_inv = gm[:, 6:7], gm[:, 7:8]

        raw = sb("raw", [P, CT, 4, W])
        Z = sb("Z", [P, CT, 2, 2, PT])
        Z3 = sb("Z3", [P, 2, PAIRS + DJ - 1])
        ytj = sb("ytj", [P, 2 * C])
        yt = ytj[0:W, :].rearrange("p (m c) -> p m c", m=2)
        junk = (raw[:, :, :, :].rearrange("p a b c -> p (a b c)"), ytj[:, :])
        s12 = sb("s12", [P, CT, 2, W])
        s3 = sb("s3", [P, PAIRS])
        s3t = sb("s3t", [PAIRS, 3, P], fp16)
        ab = sb("ab", [P, CT, P])
        ab_hi = sb("ab_hi", [P, C], fp16)
        ab_lo = sb("ab_lo", [P, C], fp16)
        w3c = sb("w3c", [P, CT, 3])
        w3h = sb("w3h", [P, CT], fp16)
        w3t = sb("w3t", [3, C], fp16)
        wt = sb("wt", [P, CT, 3])
        sm = sb("sm", [P, 4, CT])
        part = sb("part", [P, CT, NCH])
        pooled = sb("pooled", [P, CT])
        stats = sb("stats", [P, CT, NCH, 6])
        mv = sb("mv", [P, CT, 2])
        gn = sb("gn", [P, 6, CT])
        g_mean, g_dev, g_sq, g_ve, g_r, g_b = (gn[:, i, :] for i in range(6))
        al = sb("al", [P, 2, 5])
        r64 = sb("r64", [P, CT])
        y1 = sb("y1", [P, CT, H])
        ysum = sb("ysum", [P, 2, CT])
        hid = sb("hid", [HID, 1])
        wch = sb("wch", [P, 6, CT])
        alpha, beta, a3, b3, beta_o = (wch[:, i, :] for i in range(1, 6))
        tmp = sb("tmp", [P, 4, CHUNK])
        srow = tmp[0:3, :, :].rearrange("p a b -> p (a b)").bitcast(fp16)
        tok = sb("tok", [P, CT, CHUNK])
        tok_hi = sb("tok_hi", [P, CT, CHUNK], fp16)
        tok_lo = sb("tok_lo", [P, CT, CHUNK], fp16)
        qbd = sb("qbd", [P, CT, NW, 2, TOK])
        kk = sb("kk", [P, CT, CHUNK])
        vv = sb("vv", [P, NW // 2, C])
        sc = sb("sc", [P, 4, CHUNK])
        xr = sb("xr", [P, 3, CT, CHUNK])
        coef = sb("coef", [P, 4, CT])
        c_alpha, c_beta, c_a3, c_b3 = (coef[:, i, :] for i in range(4))
        prt = sb("prt", [P, 2, CHUNK])
        mx = sb("mx", [P, 4, 8])
        sums = sb("sums", [P, 4, 8])
        rec = sb("rec", [P, 4, 8])
        ot = sb("ot", [P, CT, CHUNK])

        F = ps("F", [P, 2, CHUNK])
        QP = ps("QP", [P, CHUNK])
        SP = ps("SP", [P, 2, CHUNK])
        PTR = ps("PTR", [P, CHUNK])
        O = ps("O", [P, 2, CHUNK])

        scratch_t = nc.dram_tensor("scratch_t", (P, T_ALL), fp32)
        scratch_x = nc.dram_tensor("scratch_x", (NB, C, HW), fp32)
        scratch_w = nc.dram_tensor("scratch_w", (C, C * TAPS), fp32)

        consts_in = sem("consts_in")
        zero_set = sem("zero_set")
        zero_out = sem("zero_out")
        bands_out = sem("bands_out")
        bands_in = sem("bands_in")
        wconv_in = sem("wconv_in")
        wcirc_set = sem("wcirc_set")
        wcirc_out = sem("wcirc_out")
        wrow_in = sem("wrow_in")
        bias_rev_in = sem("bias_rev_in")
        setup_max = sem("setup_max")
        setup_gmax = sem("setup_gmax")
        setup_scaled = sem("setup_scaled")
        setup_tr = sem("setup_tr")
        setup_hi = sem("setup_hi")
        setup_lo = sem("setup_lo")
        setup_exp = sem("setup_exp")
        setup_bn = sem("setup_bn")
        x_loaded = sem("x_loaded")
        dve_seq = sem("dve_seq")
        act_seq = sem("act_seq")
        pool_seq = sem("pool_seq")
        gn_stats = sem("gn_stats")
        gn_mean = sem("gn_mean")
        gn_sq = sem("gn_sq")
        gn_var = sem("gn_var")
        gn_ve = sem("gn_ve")
        gn_rstd = sem("gn_rstd")
        gn_coef = sem("gn_coef")
        g_ready = sem("g_ready")
        f_tr = sem("f_tr")
        f_max = sem("f_max")
        z_ready = sem("z_ready")
        y_done = sem("y_done")
        y_copied = sem("y_copied")
        y_tr = sem("y_tr")
        e12_ready = sem("e12_ready")
        s12_ready = sem("s12_ready")
        f_sum = sem("f_sum")
        raw_sums = sem("raw_sums")
        y3_done = sem("y3_done")
        e3_ready = sem("e3_ready")
        s3_ready = sem("s3_ready")
        s3_tr = sem("s3_tr")
        s3_split = sem("s3_split")
        srow_in = sem("srow_in")
        s3b_done = sem("s3b_done")
        s3b_used = sem("s3b_used")
        pooled_set = sem("pooled_set")
        logits_done = sem("logits_done")
        lg_ready = sem("lg_ready")
        lg_exp = sem("lg_exp")
        ab_set = sem("ab_set")
        ab_tr = sem("ab_tr")
        ab_hi_set = sem("ab_hi_set")
        ab_lo_set = sem("ab_lo_set")
        gate_done = sem("gate_done")
        gated = sem("gated")
        x1_set = sem("x1_set")
        pads_set = sem("pads_set")
        nrm_set = sem("nrm_set")
        hi_set = sem("hi_set")
        lo_set = sem("lo_set")
        conv_done = sem("conv_done")
        x2_set = sem("x2_set")
        dwt_mul = sem("dwt_mul")
        dwt_used = sem("dwt_used")
        se_y = sem("se_y")
        se_h = sem("se_h")
        se_relu = sem("se_relu")
        se_z = sem("se_z")
        se_exp = sem("se_exp")
        coef3 = sem("coef3")
        tok_set = sem("tok_set")
        tok_hi_set = sem("tok_hi_set")
        tok_lo_set = sem("tok_lo_set")
        x3_set = sem("x3_set")
        qp_done = sem("qp_done")
        qp_read = sem("qp_read")
        s_done = sem("s_done")
        s_biased = sem("s_biased")
        s_max = sem("s_max")
        s_sub = sem("s_sub")
        p_exp = sem("p_exp")
        p_rec = sem("p_rec")
        p_norm = sem("p_norm")
        pt_done = sem("pt_done")
        pt_read = sem("pt_read")
        pv_done = sem("pv_done")
        o_read = sem("o_read")
        x4_set = sem("x4_set")
        xr_in = [sem(f"xr_in{i}") for i in range(3)]
        x2_stored = [sem(f"x2_stored{i}") for i in range(4)]
        x_next = sem("x_next")
        xr_first = sem("xr_first")
        stored = [sem(f"stored{i}") for i in range(3)]

        class Chain:

            def __init__(self, eng, s):
                self.eng, self.s, self.n = eng, s, 0

            def link(self, ins):
                self.n += 1
                ins.then_inc(self.s, 1)
                self.eng.wait_ge(self.s, self.n)

        def dram(t, offset, dims):
            return bass.AP(t.tensor if isinstance(t, bass.AP) else t, offset, dims)

        def clear_semaphores():
            with nc.Block() as block:
                @block.gpsimd
                def _(pool):
                    for s in sems[0::4]:
                        pool.sem_clear(s)

                @block.scalar
                def _(act):
                    for s in sems[1::4]:
                        act.sem_clear(s)

                @block.vector
                def _(dve):
                    for s in sems[2::4]:
                        dve.sem_clear(s)

                @block.tensor
                def _(pe):
                    for s in sems[3::4]:
                        pe.sem_clear(s)

        WB = X[:, :, :].rearrange("p t n -> p (t n)")[:, 0:BMAX * 2 * BMAX * TAPS]
        WR = X[:, :, :].rearrange("p t n -> p (t n)")[:, 0:CT * C * TAPS].rearrange("p (t n) -> p t n", t=CT)
        acc = Gn.rearrange("p t n -> p (t n)")[:, 0:BMAX * 2 * BMAX * TAPS]
        tc = toep[:, :, :, :].rearrange("p a b c -> p (a b c)")[:, 0:BMAX * BMAX * TAPS]
        qkv_f = Gn.rearrange("p t n -> p (t n)")[:, 0:CT * 3 * C].rearrange("p (t n) -> p t n", t=CT)
        tcr = Gn.rearrange("p t n -> p (t n)")[:, 4608:4608 + 2304]
        zeros = Gn.rearrange("p t n -> p (t n)")[:, 0:T_ALL]
        bias_rev = tok[:, :, :].rearrange("p t n -> p (t n)")[:, 0:2 * CT * TOK].rearrange(
            "p (s t m) -> p s t m", s=2, t=CT)
        mask = tmp[:, 0, 0:4 * TOK].rearrange("p (y m) -> p y m", y=4)

        with nc.Block() as block:
            small = [(gavg[:, :], c_gavg), (ident[:, :], c_ident), (ind[:, :], c_ind), (ones3[:, :], c_ones3),
                     (half[:, :], c_half), (w2[:, :], w2t),
                     (w1[:, :, :], w1t.rearrange("(t p) n -> p t n", p=P)),
                     (wo[:, :, :], w_o.rearrange("(t p) n -> p t n", p=P)),
                     (bq[:, :], b_qkv),
                     (bo[:, :], b_o),
                     (bnp[:, :, :], dram(bn, 0, [[0, P], [3, 4], [1, 3]])),
                     (al[:, 0, :], dram(alphas, 0, [[0, P], [1, 5]])),
                     (uw[:, :], dram(c_u, 0, [[0, P], [1, W]])),
                     (mask, c_mask)]

            @block.sync
            def _(sp):
                for q in range(C // BMAX):
                    sp.dma_start(WB[8 * q:8 * q + 8, :].rearrange("p (r n) -> p r n", r=BMAX),
                                 dram(w_conv, q * BMAX * C * TAPS,
                                      [[2 * BMAX * TAPS, 8], [C * TAPS, BMAX], [1, 2 * BMAX * TAPS]])
                                 ).then_inc(wconv_in, 16)
                for dst, src in small:
                    sp.dma_start(dst, src).then_inc(consts_in, 16)
                sp.wait_ge(zero_set, 1)
                sp.dma_start(scratch_t[:, :], zeros).then_inc(zero_out, 16)
                sp.wait_ge(zero_out, 16)
                n = 0
                for m, k in enumerate((k_cw, k_hc)):
                    sp.dma_start(dram(scratch_t, T_CW + m * NM * BAND, [[T_ALL + 1, P], [BAND, NM], [1, KS]]),
                                 dram(k, 0, [[0, P], [KS, NM], [1, KS]])).then_inc(bands_out, 16)
                    n += 1
                for a in range(2):
                    for b in range(2):
                        for dj in range(DJ):
                            kh = 2 * (dj - 2) + a - b + PAD
                            if 0 <= kh < KS:
                                sp.dma_start(dram(scratch_t, a * W * T_ALL + T_HW + dj * 2 * PT + b * PT,
                                                  [[T_ALL + 1, W], [DJ * 2 * PT, 2], [1, KS]]),
                                             dram(k_hw, kh * KS, [[0, W], [KS * KS, 2], [1, KS]])
                                             ).then_inc(bands_out, 16)
                                n += 1
                sp.dma_start(dram(scratch_t, T_1D + P - PAD, [[T_ALL + 1, P], [W1D, 3], [1, KS]]),
                             dram(k_1d, 0, [[0, P], [KS, 3], [1, KS]])).then_inc(bands_out, 16)
                n += 1
                sp.wait_ge(bands_out, 16 * n)
                sp.wait_ge(wcirc_set, 1)
                for q in range(C // BMAX):
                    sp.dma_start(dram(scratch_w, q * BMAX * C * TAPS,
                                      [[2 * BMAX * TAPS, 8], [C * TAPS, BMAX], [1, 2 * BMAX * TAPS]]),
                                 acc[8 * q:8 * q + 8, :].rearrange("p (r n) -> p r n", r=BMAX)
                                 ).then_inc(wcirc_out, 16)
                sp.wait_ge(wcirc_out, 16 * (C // BMAX))
                sp.dma_start(WR, scratch_w[:, :].rearrange("(t p) n -> p t n", p=P)).then_inc(wrow_in, 16)
                sp.dma_start(qkv_f, w_qkv.rearrange("(t p) n -> p t n", p=P)).then_inc(wrow_in, 16)
                sp.dma_start(toep[:, :, :, :].rearrange("p a b c -> p (a b c)"),
                             scratch_t[:, T_CW:T_HW]).then_inc(bands_in, 16)
                sp.dma_start(t_hw[:, :, :, :],
                             scratch_t[:, T_HW:T_1D].rearrange("p (m a w) -> p m a w", a=2, w=PT)[:, :, :, PAD:PAD + W]
                             ).then_inc(bands_in, 16)
                sp.dma_start(t_1d[:, :, :], scratch_t[:, T_1D:T_ALL].rearrange("p (k n) -> p k n", k=3)
                             ).then_inc(bands_in, 16)
                sp.wait_ge(bands_in, 48)

            @block.gpsimd
            def _(pool):
                seq = Chain(pool, pool_seq)
                pool.memset(zeros, 0.0).then_inc(zero_set, 1)
                pool.memset(zrow[:, :], 0.0)
                pool.memset(neg_half[:, :], -0.5)
                pool.memset(Z[:, :, :, :, :], 0.0)
                pool.memset(Z3[:, :, :], 0.0)
                n = 0
                for h in range(HEADS):
                    cg, hs, h2 = h // 4, h // 2 % 2, h % 2
                    for yq in range(WS):
                        pool.dma_start(bias_rev[64 * h2 + 8 * yq:64 * h2 + 8 * yq + 8, hs, cg, :]
                                       .rearrange("p (y x) -> p y x", y=WS),
                                       dram(rel_t, h * (2 * WS - 1) ** 2 + yq * (2 * WS - 1),
                                            [[1, WS], [2 * WS - 1, WS], [1, WS]])).then_inc(bias_rev_in, 16)
                pool.wait_ge(consts_in, 16 * len(small))
                seq.link(pool.tensor_scalar(bn_s[:, :], bnp[:, 3, :], EPS, None, ALU.add))
                seq.link(pool.memset(gm[:, 0:3], -0.5))
                seq.link(pool.tensor_tensor(bn_s[:, :], bn_s[:, :], gm[:, 0:3], ALU.pow))
                seq.link(pool.tensor_tensor(bn_s[:, :], bn_s[:, :], bnp[:, 0, :], ALU.mult))
                seq.link(pool.tensor_tensor(bn_b[:, :], bn_s[:, :], bnp[:, 2, :], ALU.mult))
                seq.link(pool.tensor_tensor(bn_b[:, :], bnp[:, 1, :], bn_b[:, :], ALU.subtract))
                pool.tensor_scalar(bn_b[:, :], bn_b[:, :], 0.5, None, ALU.mult)
                pool.tensor_scalar(bn_s[:, :], bn_s[:, :], 0.5, None, ALU.mult).then_inc(setup_bn, 1)
                for i in range(2):
                    pool.wait_ge(setup_max, i + 1)
                    pool.partition_all_reduce(gm[:, 2 + i:3 + i], gm[:, i:i + 1], P, ABSMAX).then_inc(setup_gmax, 1)

            @block.scalar
            def _(act):
                act.wait_ge(setup_exp, 1)
                S.activation(al[:, 0, :], al[:, 1, :], ACT.Exp).then_inc(act_seq, 1)
                for n in range(18):
                    act.wait_ge(setup_tr, n + 1)
                    ti, tap = n // 9, n % 9
                    S.activation(cw_hi[:, ti, tap, :], F[:, n % 2, 0:C], ACT.Copy).then_inc(setup_hi, 1)

            @block.vector
            def _(dve):
                seq = Chain(dve, dve_seq)
                dve.wait_ge(consts_in, 16 * len(small))
                seq.link(V.reduce_max(sm[:, 0, 0:1], al[:, 0, :], AX.X))
                V.tensor_scalar(al[:, 1, :], al[:, 0, :], sm[:, 0, 0:1], None, ALU.subtract).then_inc(setup_exp, 1)
                dve.wait_ge(act_seq, 1)
                seq.link(V.reduce_sum(sm[:, 1, 0:1], al[:, 0, :], AX.X))
                seq.link(V.reciprocal(sm[:, 2, 0:1], sm[:, 1, 0:1]))
                seq.link(V.tensor_scalar(al[:, 1, :], al[:, 0, :], sm[:, 2, 0:1], None, ALU.mult))
                dve.wait_ge(wconv_in, 16 * (C // BMAX))
                dve.wait_ge(zero_out, 16)
                seq.link(V.tensor_scalar(acc, WB, al[:, 1, 0:1], None, ALU.mult))
                for n, b in enumerate(BLOCKS):
                    size = BMAX * 2 * BMAX // b * TAPS
                    rb, pc = BMAX // b, 2 * BMAX // b

                    def blocks(ap, j, lo, count):
                        v = ap.rearrange("p (R r q c) -> p R r q c", R=rb, r=b, q=pc)
                        return v[:, :, j, :, lo * TAPS:(lo + count) * TAPS]

                    def diag(ap, lo, count):
                        v = ap[:, 0:size].rearrange("p (R q c) -> p R q c", R=rb, q=pc)
                        return v[:, :, :, lo * TAPS:(lo + count) * TAPS]

                    seq.link(V.tensor_copy(diag(tc, 0, b), blocks(WB, 0, 0, b)))
                    for j in range(1, b):
                        V.tensor_tensor(diag(tc, 0, b - j), diag(tc, 0, b - j), blocks(WB, j, j, b - j), ALU.add)
                        seq.link(V.tensor_tensor(diag(tc, b - j, j), diag(tc, b - j, j), blocks(WB, j, 0, j), ALU.add))
                    for i in range(b):
                        last = V.tensor_scalar(diag(tcr, i, 1), diag(tc, (-i) % b, 1), al[:, 1, n + 1:n + 2],
                                               1.0 / b, ALU.mult, ALU.mult)
                    seq.link(last)
                    for r in range(b):
                        if r:
                            V.tensor_tensor(blocks(acc, r, 0, r), blocks(acc, r, 0, r), diag(tcr, b - r, r), ALU.add)
                        last = V.tensor_tensor(blocks(acc, r, r, b - r), blocks(acc, r, r, b - r),
                                               diag(tcr, 0, b - r), ALU.add)
                    seq.link(last)
                V.memset(sm[:, 3, :], 0.0).then_inc(wcirc_set, 1)
                dve.wait_ge(bias_rev_in, 16 * HEADS * WS)
                for y in range(4):
                    for hs in range(2):
                        for cg in range(CT):
                            V.tensor_tensor(bias[:, y, hs, cg, :], bias_rev[:, hs, cg, ::-1], mask[:, y, :], ALU.add)
                dve.wait_ge(wrow_in, 32)
                dve.wait_ge(setup_bn, 1)
                V.tensor_reduce(gm[:, 0:1], WR, AX.XY, ALU.max, apply_absolute_value=True).then_inc(setup_max, 1)
                V.tensor_reduce(gm[:, 1:2], qkv_f, AX.XY, ALU.max, apply_absolute_value=True).then_inc(setup_max, 1)
                dve.wait_ge(setup_gmax, 2)
                seq.link(V.tensor_scalar(gm[:, 2:4], gm[:, 2:4], 1e-30, None, ALU.max))
                seq.link(V.reciprocal(gm[:, 4:6], gm[:, 2:4]))
                V.tensor_scalar(gm[:, 6:8], gm[:, 2:4], 1.0 / FULL, None, ALU.mult)
                seq.link(V.tensor_scalar(gm[:, 4:6], gm[:, 4:6], FULL, None, ALU.mult))
                V.tensor_scalar(WR, WR, gm[:, 4:5], None, ALU.mult).then_inc(setup_scaled, 1)
                seq.link(V.tensor_scalar(qkv_f, qkv_f, gm[:, 5:6], None, ALU.mult))
                seq.link(V.tensor_copy(qkv_hi[:, :, :], qkv_f))
                V.tensor_tensor(qkv_lo[:, :, :], qkv_f, qkv_hi[:, :, :], ALU.subtract)
                seq.link(V.tensor_scalar(q_scale[:, :], half[:, :], qkv_inv, DH ** -0.5, ALU.mult, ALU.mult))
                for cg in range(CT):
                    V.tensor_scalar(q_bias[:, cg, :], half[:, :], bq[:, cg:cg + 1], DH ** -0.5, ALU.mult, ALU.mult)
                for n in range(18):
                    ti, tap = n // 9, n % 9
                    dve.wait_ge(setup_hi, n + 1)
                    V.tensor_tensor(cw_lo[:, ti, tap, :], F[:, n % 2, 0:C], cw_hi[:, ti, tap, :],
                                    ALU.subtract).then_inc(setup_lo, 1)
                dve.wait_ge(setup_tr, 19)
                V.tensor_tensor(bvo[:, :], QP[:, 0:CT], bo[:, :], ALU.add)

            @block.tensor
            def _(pe):
                pe.wait_ge(setup_scaled, 1)
                pe.wait_ge(consts_in, 16 * len(small))
                rows = WR.rearrange("p t (i k) -> p t i k", k=TAPS)
                for n in range(18):
                    ti, tap = n // 9, n % 9
                    if n >= 2:
                        pe.wait_ge(setup_lo, n - 1)
                    for to in range(CT):
                        last = T.transpose(F[:, n % 2, P * to:P * to + P], rows[:, to, P * ti:P * ti + P, tap],
                                           ident[:, :])
                    last.then_inc(setup_tr, 1)
                for co in range(CT):
                    for ci in range(CT):
                        last = T.matmul(QP[:, co:co + 1], wo[:, ci, P * co:P * co + P], bq[:, 4 + ci:5 + ci],
                                        start=(ci == 0), stop=(ci == CT - 1))
                last.then_inc(setup_tr, 1)

        FRONT = ([f"stats{i}" for i in range(4)] + ["norm0a", "norm0b", "norm0c"] + [f"reduce{i}" for i in range(8)]
                 + ["zpool", "hwconv", "hwgate", "hwrows"] + [f"band{i}" for i in range(4)]
                 + ["bandcopy", "bandturn"] + [f"hwmean{k}" for k in range(NCH)]
                 + ["logits", "mix", "mixturn"] + [f"gate{n}" for n in range(CT * NCH + 2)]
                 + ["norm1a", "norm1b", "norm1c"] + [f"split{n}" for n in range(4)]
                 + [f"conv{n}.{i}" for n in range(CT * NCH) for i in range(6)]
                 + ["norm2a", "norm2b", "norm2c", "squeeze", "excite", "norm3a", "norm3b", "norm3c", "coefs"])
        ATT = [f"p{i}" for i in range(6)] + [f"{c}{r}" for r in range(NW) for c in "CDEFGHIJK"] + [
            f"L{NW - 1}", f"M{NW - 1}"]
        FILLS = ["q0.0", "q1.0", "k0.0", "k1.0"]
        for r in range(NW):
            for c in ("v0", "v1", "p0", "p1"):
                if c[0] == "v":
                    FILLS.append(f"{c}.{r}")
                elif r:
                    FILLS.append(f"{c}.{r - 1}")
            if r + 1 < NW:
                FILLS += [f"{c}.{r + 1}" for c in ("q0", "q1", "k0", "k1")]
        FILLS += [f"p0.{NW - 1}", f"p1.{NW - 1}"]
        FILL = {name: n for n, name in enumerate(FILLS)}

        def weight(step):
            if step.startswith("conv"):
                return W_CONV
            if step[:4] in ("norm", "sque", "exci", "coef"):
                return W_NORM
            if step.startswith("reduce"):
                return W_RED
            return W_L0

        def merged(has_front, has_att):
            if not has_front:
                return [("att", a) for a in ATT]
            if not has_att:
                return [("front", f) for f in FRONT]
            total = sum(weight(f) for f in FRONT)
            order, done, k = [], 0.0, 0
            for f in FRONT:
                order.append(("front", f))
                done += weight(f)
                while k < len(ATT) and k < done / total * len(ATT):
                    order.append(("att", ATT[k]))
                    k += 1
            return order

        def play(order, front, att):
            for kind, name in order:
                said = next(front if kind == "front" else att)
                assert said == name, (said, name)

        def row_pieces(r):
            return [(0, WS, WS * r + SHIFT)] if r < NW - 1 else [(0, SHIFT, WS * r + SHIFT), (SHIFT, SHIFT, 0)]

        def turn(image_f, image_a, prefetch):
          has_front, has_att = image_f is not None, image_a is not None
          order = merged(has_front, has_att)
          with nc.Block() as block:
            Zv = Z[:, :, :, :, :]

            def chunk(n):
                k, t = divmod(n, CT)
                return k, t, slice(CHUNK * k, CHUNK * k + CHUNK)

            def rows_view(ap):
                return ap.rearrange("p (r c) -> p r c", c=W)

            def keyed(ap):
                return ap.rearrange("p (n m) -> p n m", m=TOK)

            @block.sync
            def _(sp):
                def front():
                    for f in FRONT:
                        if f == "hwrows":
                            sp.wait_ge(s3_split, 1)
                            for k in range(3):
                                sp.dma_start(srow[k:k + 1, :].rearrange("k (j p) -> k j p", p=P), s3t[:, k, :]
                                             ).then_inc(srow_in, 16)
                        if f.startswith("conv") and f.endswith(".5"):
                            n = int(f[4:-2]) - 2
                            if n >= 0:
                                store_x2(n)
                        if f == "norm2a":
                            store_x2(CT * NCH - 2)
                            store_x2(CT * NCH - 1)
                        if f == "norm2b" and prefetch is not None:
                            fetch(CT * NCH - 2)
                            fetch(CT * NCH - 1)
                        if f == "norm3a":
                            for i in range(4):
                                sp.wait_ge(x2_stored[i], 16 * CT * NCH // 4)
                            first_rows()
                        if f == "coefs":
                            if prefetch is not None:
                                sp.wait_ge(x_next, 16 * CT * NCH)
                        yield f

                def store_x2(n):
                    k, t, px = chunk(n)
                    sp.wait_ge(x2_set, n + 1)
                    sp.dma_start(scratch_x[bass.ds(image_f, 1), P * t:P * t + P, px].rearrange("b p n -> p (b n)"),
                                 X[:, t, px]).then_inc(x2_stored[n % 4], 16)
                    if prefetch is not None and n >= 2 and n < CT * NCH - 1:
                        fetch(n - 2)
                    if prefetch is not None and n == CT * NCH - 1:
                        fetch(n - 2)

                def fetch(n):
                    k, t, px = chunk(n)
                    sp.wait_ge(x2_stored[n % 4], 16 * (n // 4 + 1))
                    sp.wait_ge(dwt_used, n + 1)
                    sp.dma_start(X[:, t, px], x[bass.ds(prefetch, 1), P * t:P * t + P, px].rearrange("b p n -> p (b n)")
                                 ).then_inc(x_next, 16)

                def first_rows():
                    if has_att:
                        sp.wait_ge(stored[0], 16 * len(range(0, NW, 3)))
                    sp.dma_start(xr[:, 0, :, :], scratch_x[bass.ds(image_f, 1), :, W * SHIFT:W * (SHIFT + WS)]
                                 .rearrange("b (t p) n -> p (b t) n", p=P)).then_inc(xr_first, 16)

                def load_rows(r):
                    if r >= 3:
                        sp.wait_ge(stored[r % 3], 16 * (r // 3))
                    for i0, n, row in row_pieces(r):
                        sp.dma_start(xr[:, r % 3, :, W * i0:W * (i0 + n)],
                                     scratch_x[bass.ds(image_a, 1), :, W * row:W * (row + n)]
                                     .rearrange("b (t p) n -> p (b t) n", p=P)).then_inc(xr_in[r % 3], 16)

                def store_rows(r):
                    sp.wait_ge(x4_set, CT * (r + 1))
                    for i0, n, row in row_pieces(r):
                        sp.dma_start(out[bass.ds(image_a, 1), :, W * row:W * (row + n)]
                                     .rearrange("b (t p) n -> p (b t) n", p=P),
                                     xr[:, r % 3, :, W * i0:W * (i0 + n)]).then_inc(stored[r % 3], 16)

                def att():
                    for name in ATT:
                        c, r = name[0], int(name[1:])
                        if name == "p0":
                            load_rows(1)
                        if c == "G" and r:
                            store_rows(r - 1)
                        if c == "I" and r + 2 < NW:
                            load_rows(r + 2)
                        if c == "M":
                            store_rows(r)
                            for j in range(3):
                                sp.wait_ge(stored[j], 16 * (len(range(j, NW, 3)) + (j == (NW - 1) % 3)))
                        yield name

                play(order, front(), att())
                if has_front:
                    sp.wait_ge(xr_first, 16)

            @block.gpsimd
            def _(pool):
                seq = Chain(pool, pool_seq)

                def front():
                    sums_left = (op for t in range(CT) for rows in range(2) for op in row_or_column_sums(t, rows))
                    added = 0

                    def rstd(n):
                        pool.wait_ge(gn_ve, n + 1)
                        G.tensor_tensor(g_r, g_ve, neg_half[:, :], ALU.pow).then_inc(gn_rstd, 1)

                    for f in FRONT:
                        if f in SUM_STEPS:
                            share = 2 * CT * SUM_OPS * (SUM_STEPS.index(f) + 1) // len(SUM_STEPS)
                            while added < share:
                                next(sums_left)
                                added += 1
                        if f in ("norm0b", "norm1b", "norm2b", "norm3b"):
                            rstd(int(f[4]))
                        if f.startswith("gate"):
                            n = int(f[4:]) - 1
                            if 0 <= n < CT * NCH:
                                k, t, px = chunk(n)
                                pool.wait_ge(gated, n + 1)
                                G.tensor_tensor(X[:, t, px], X[:, t, px], Gn[:, t, px], ALU.add).then_inc(x1_set, 1)
                            if n == CT * NCH:
                                pool.wait_ge(x1_set, CT * NCH)
                                for l in range(2):
                                    for t in range(CT):
                                        G.memset(halves[:, l, t, 0::HP - 1, :], 0.0)
                                        last = G.memset(halves[:, l, t, 1:HP - 1, 0::HP - 1], 0.0)
                                last.then_inc(pads_set, 1)
                        if f.startswith("conv") and f.endswith(".1"):
                            weigh_rows(int(f[4:-2]) - 1)
                        if f == "norm2a":
                            weigh_rows(CT * NCH - 1)
                        yield f

                def row_or_column_sums(t, rows):
                    src = X[:, t, :].rearrange("p (h w) -> p h w", w=W)
                    flat = tmp[:, 2:4, :].rearrange("p a b -> p (a b)")
                    n = W // 4
                    if rows:
                        part_sum = flat.rearrange("p (h w) -> p h w", w=n)
                        slabs = [src[:, :, n * i:n * i + n] for i in range(4)]
                    else:
                        part_sum = flat.rearrange("p (h w) -> p h w", w=W)
                        slabs = [src[:, n * i:n * i + n, :] for i in range(4)]
                    seq.link(G.tensor_tensor(part_sum, slabs[0], slabs[1], ALU.add))
                    yield
                    seq.link(G.tensor_tensor(part_sum, part_sum, slabs[2], ALU.add))
                    yield
                    seq.link(G.tensor_tensor(part_sum, part_sum, slabs[3], ALU.add))
                    yield
                    while n > 2:
                        n //= 2
                        low, high = ((part_sum[:, :, 0:n], part_sum[:, :, n:2 * n]) if rows else
                                     (part_sum[:, 0:n, :], part_sum[:, n:2 * n, :]))
                        seq.link(G.tensor_tensor(low, low, high, ALU.add))
                        yield
                    low, high = ((part_sum[:, :, 0], part_sum[:, :, 1]) if rows else
                                 (part_sum[:, 0, :], part_sum[:, 1, :]))
                    G.tensor_tensor(raw[:, t, 2 * rows + 1, :], low, high, ALU.add).then_inc(raw_sums, 1)
                    pool.wait_ge(raw_sums, 2 * t + rows + 1)
                    yield

                def weigh_rows(n):
                    if n < 0:
                        return
                    k, t, px = chunk(n)
                    pool.wait_ge(x2_set, n + 1)
                    if n >= 2:
                        pool.wait_ge(dwt_used, n - 1)
                    G.tensor_tensor(rows_view(tmp[:, 2 + n % 2, :]), rows_view(X[:, t, px]),
                                    uw[:, :].unsqueeze(1).to_broadcast([P, ROWS, W]), ALU.mult).then_inc(dwt_mul, 1)

                def center(u):
                    pool.wait_ge(s_max, u + 1)
                    G.tensor_tensor(keyed(sc[:, u % 4, :]), keyed(sc[:, u % 4, :]),
                                    mx[:, u % 4, :].unsqueeze(2).to_broadcast([P, 8, TOK]),
                                    ALU.subtract).then_inc(s_sub, 1)

                def normalise(u):
                    pool.wait_ge(p_rec, u + 1)
                    G.tensor_tensor(keyed(sc[:, u % 4, :]), keyed(sc[:, u % 4, :]),
                                    rec[:, u % 4, :].unsqueeze(2).to_broadcast([P, 8, TOK]),
                                    ALU.mult).then_inc(p_norm, 1)

                def att():
                    for name in ATT:
                        c, u = name[0], 4 * int(name[1:])
                        if c in "DEFG":
                            center(u + "DEFG".index(c))
                        if c in "EFGH":
                            normalise(u + "EFGH".index(c))
                        yield name

                play(order, front(), att())

            @block.scalar
            def _(act):
                def front():
                    for f in FRONT:
                        if f.startswith("reduce") and int(f[6:]) < 4:
                            q = int(f[6:])
                            act.wait_ge(gn_coef, 1)
                            for t in range(CT):
                                piece = slice(HW // 4 * q, HW // 4 * (q + 1))
                                S.activation(Gn[:, t, piece], X[:, t, piece], ACT.Identity, bias=g_b[:, t:t + 1],
                                             scale=g_r[:, t:t + 1]).then_inc(g_ready, 1)
                        if f.startswith("reduce"):
                            channel_means(int(f[6:]))
                        if f == "hwgate":
                            act.wait_ge(y3_done, 1)
                            S.activation(s3[:, :], F[:, 1, 0:PAIRS], ACT.Tanh, bias=bn_b[:, 2:3],
                                         scale=bn_s[:, 2:3]).then_inc(e3_ready, 1)
                        if f == "bandcopy":
                            act.wait_ge(y_done, 2)
                            for m in range(2):
                                S.activation(yt[:, m, :], F[0:W, m, PAD:PAD + C], ACT.Copy).then_inc(y_copied, 1)
                        if f == "bandturn":
                            act.wait_ge(y_tr, 1)
                            for m in range(2):
                                S.activation(s12[:, :, m, :],
                                             F[:, 0, 0:4 * W].rearrange("p (t m w) -> p t m w", t=CT, m=2)[:, :, m, :],
                                             ACT.Tanh, bias=bn_b[:, m:m + 1], scale=bn_s[:, m:m + 1]
                                             ).then_inc(e12_ready, 1)
                        if f == "mix":
                            act.wait_ge(lg_ready, 1)
                            S.activation(wt[:, :, :], wt[:, :, :], ACT.Exp).then_inc(lg_exp, 1)
                        if f == "mixturn":
                            act.wait_ge(ab_tr, 1)
                            S.activation(ab_hi[:, :], F[:, 0, 0:C], ACT.Copy).then_inc(ab_hi_set, 1)
                            S.activation(w3t[:, :], F[0:3, 1, 0:C], ACT.Copy).then_inc(ab_hi_set, 1)
                        if f.startswith("split"):
                            split(int(f[5:]))
                        if f.startswith("conv") and f.endswith(".0") and int(f[4:-2]) + 4 < CT * NCH:
                            split(int(f[4:-2]) + 4)
                        if f == "excite":
                            act.wait_ge(se_z, 1)
                            S.activation(wch[:, 0, :], F[:, 1, 0:CT], ACT.Tanh, scale=0.5).then_inc(se_exp, 1)
                        yield f

                def channel_means(i):
                    for jj in (2 * i, 2 * i + 1):
                        act.wait_ge(f_max, jj + 1)
                        if jj >= 2:
                            act.wait_ge(f_sum, jj - 1)
                        for j in range(2):
                            last = S.activation(tmp[:, jj % 2, C * j:C * j + C], F[:, jj % 2, C * j:C * j + C], ACT.Copy,
                                                scale=1.0 / C, accum_out=Z3[:, 1, 2 + 2 * jj + j:3 + 2 * jj + j])
                        last.then_inc(f_sum, 1)

                def split(n):
                    k, t, px = chunk(n)
                    if n == 0:
                        act.wait_ge(gn_coef, 2)
                        act.wait_ge(pads_set, 1)
                    if n >= 2:
                        act.wait_ge(lo_set, n - 1)
                    S.activation(tmp[:, n % 2, :], X[:, t, px], ACT.Identity, bias=g_b[:, t:t + 1],
                                 scale=g_r[:, t:t + 1]).then_inc(nrm_set, 1)
                    S.activation(halves[:, 0, t, 1 + ROWS * k:1 + ROWS * k + ROWS, 1:1 + W], rows_view(X[:, t, px]),
                                 ACT.Identity, bias=g_b[:, t:t + 1], scale=g_r[:, t:t + 1]).then_inc(hi_set, 1)

                def tokens(r, t):
                    if r:
                        act.wait_ge(tok_lo_set, CT * r)
                        act.wait_ge(qp_done, FILL[f"v1.{r - 1}"] + 1)
                    if t == 0 and r:
                        act.wait_ge(xr_in[r % 3], 16 * (r // 3 + (r % 3 > 0)) + 16 * (r == NW - 1))
                    src = rows_view(xr[:, r % 3, t, :])
                    dst = rows_view(tok[:, t, :])
                    high = tok_hi[:, t, :].rearrange("p (w i j) -> p w i j", w=NW, i=WS)
                    kw = dict(bias=c_b3[:, t:t + 1], scale=c_a3[:, t:t + 1])
                    S.activation(dst[:, :, 0:W - SHIFT], src[:, :, SHIFT:W], ACT.Identity, **kw)
                    S.activation(dst[:, :, W - SHIFT:W], src[:, :, 0:SHIFT], ACT.Identity, **kw).then_inc(tok_set, 1)
                    act.wait_ge(tok_set, CT * r + t + 1)
                    S.activation(high, tok[:, t, :].rearrange("p (i w j) -> p w i j", w=NW, i=WS),
                                 ACT.Copy).then_inc(tok_hi_set, 1)

                def residual(r, t):
                    S.activation(xr[:, r % 3, t, :], xr[:, r % 3, t, :], ACT.Identity, bias=c_beta[:, t:t + 1],
                                 scale=c_alpha[:, t:t + 1]).then_inc(x3_set, 1)

                def evacuate(name):
                    kind, r = name.split(".")
                    r, i = int(r), int(kind[1])
                    act.wait_ge(qp_done, FILL[name] + 1)
                    if kind[0] == "q":
                        if r:
                            act.wait_ge(s_done, 4 * r)
                        by_win = QP[:, :].rearrange("p (w n) -> p w n", n=TOK)
                        for h2 in range(2):
                            last = S.activation(qbd[:, i, :, h2, :], by_win, ACT.Identity, bias=q_bias[:, i, h2:h2 + 1],
                                                scale=q_scale[:, h2:h2 + 1])
                    elif kind[0] == "k":
                        last = S.activation(kk[:, i, :], QP[:, :], ACT.Identity, bias=bq[:, 2 + i:3 + i], scale=qkv_inv)
                    else:
                        if r:
                            act.wait_ge(pv_done, 4 * r)
                        last = S.activation(vv[:, 2 * i:2 * i + 2, :].rearrange("p a c -> p (a c)"), QP[:, :],
                                            ACT.Copy, scale=qkv_inv)
                    last.then_inc(qp_read, 1)

                def exponential(u):
                    act.wait_ge(s_sub, u + 1)
                    S.activation(sc[:, u % 4, :], sc[:, u % 4, :], ACT.Exp).then_inc(p_exp, 1)

                def turned(u):
                    act.wait_ge(pt_done, u + 1)
                    if u >= 2:
                        act.wait_ge(pv_done, u - 1)
                    S.activation(prt[:, u % 2, :], PTR[:, :], ACT.Copy).then_inc(pt_read, 1)

                def att():
                    for name in ATT:
                        c, r = name[0], int(name[1:])
                        u, more = 4 * r, r + 1 < NW
                        if c == "p":
                            if r < 2:
                                tokens(0, r)
                            else:
                                evacuate(FILLS[r - 2])
                                if r < 2 + CT:
                                    residual(0, r - 2)
                        if c in "DEFG":
                            exponential(u + "DEFG".index(c))
                        if c in "CD":
                            evacuate(f"v{'CD'.index(c)}.{r}")
                        if c in "GHIJ":
                            turned(u + "GHIJ".index(c))
                        if c in "EF" and more:
                            tokens(r + 1, "EF".index(c))
                        if c in "HIJK" and more:
                            evacuate(("q0", "q1", "k0", "k1")["HIJK".index(c)] + f".{r + 1}")
                        if c in "IJ" and more:
                            residual(r + 1, "IJ".index(c))
                        if c == "K":
                            act.wait_ge(pv_done, u + 4)
                            if r:
                                act.wait_ge(qp_done, FILL[f"p1.{r - 1}"] + 1)
                            for par in range(2):
                                last = S.activation(
                                    ot[:, :, :].rearrange("p g (c w n) -> p g c w n", w=2, n=TOK)[:, :, :, par, :],
                                    O[:, par, :].rearrange("p (g c n) -> p g c n", g=CT, n=TOK), ACT.Copy)
                            last.then_inc(o_read, 1)
                        yield name

                play(order, front(), att())

            @block.vector
            def _(dve):
                seq = Chain(dve, dve_seq)

                def norm_a(n):
                    dve.wait_ge(gn_mean, n + 1)
                    seq.link(V.tensor_copy(g_mean, F[:, 0, 0:CT]))
                    seq.link(V.tensor_tensor(g_dev, mv[:, :, 0], g_mean, ALU.subtract))
                    seq.link(V.tensor_tensor(g_sq, g_dev, g_dev, ALU.mult))
                    V.tensor_tensor(g_sq, g_sq, mv[:, :, 1], ALU.add).then_inc(gn_sq, 1)

                def norm_b(n):
                    dve.wait_ge(gn_var, n + 1)
                    V.tensor_scalar(g_ve, F[:, 1, 0:CT], EPS, None, ALU.add).then_inc(gn_ve, 1)

                def norm_c(n):
                    dve.wait_ge(gn_rstd, n + 1)
                    V.scalar_tensor_tensor(g_b, g_mean, -1.0, g_r, ALU.mult, ALU.mult).then_inc(gn_coef, 1)

                def chunk_stats(n):
                    k, t, px = chunk(n)
                    return V.bn_stats(stats[:, t, k, :], X[:, t, px])

                def moments():
                    for t in range(CT):
                        last = V.bn_aggr(mv[:, t, :], stats[:, t, :, :].rearrange("p k s -> p (k s)"))
                    return last

                def reduce(i):
                    t, kind, part = i // 8, i // 4 % 2, slice(W // 4 * (i % 4), W // 4 * (i % 4 + 1))
                    view = X[:, t, :].rearrange("p (h w) -> p h w" if kind else "p (h w) -> p w h", w=W)
                    return V.tensor_reduce(raw[:, t, 2 * kind, part], view[:, part, :], AX.X, ALU.max)

                def front():
                    for i in range(4):
                        for n in range(4 * i, 4 * i + 4):
                            last = chunk_stats(n)
                        if i == 3:
                            seq.link(last)
                            moments().then_inc(gn_stats, 1)
                        yield f"stats{i}"
                    norm_a(0)
                    yield "norm0a"
                    norm_b(0)
                    yield "norm0b"
                    norm_c(0)
                    yield "norm0c"
                    for i in range(8):
                        for jj in (2 * i, 2 * i + 1):
                            dve.wait_ge(f_tr, jj + 1)
                            V.tensor_reduce(Z3[:, 0, 2 + 2 * jj:4 + 2 * jj],
                                            F[:, jj % 2, :].rearrange("p (j c) -> p j c", j=2), AX.X,
                                            ALU.max).then_inc(f_max, 1)
                            last = reduce(jj)
                            if jj == PAIRS // 2 - 1:
                                seq.link(last)
                        yield f"reduce{i}"
                    dve.wait_ge(gn_coef, 1)
                    seq.link(V.tensor_scalar(r64[:, :], g_r, 1.0 / W, None, ALU.mult))
                    dve.wait_ge(raw_sums, 2 * CT)
                    for t in range(CT):
                        V.tensor_scalar(Zv[:, t, :, 0, PAD:PAD + W], raw[:, t, 0::2, :], g_r[:, t:t + 1],
                                        g_b[:, t:t + 1], ALU.mult, ALU.add)
                        last = V.tensor_scalar(Zv[:, t, :, 1, PAD:PAD + W], raw[:, t, 1::2, :], r64[:, t:t + 1],
                                               g_b[:, t:t + 1], ALU.mult, ALU.add)
                    last.then_inc(z_ready, 1)
                    yield "zpool"
                    yield "hwconv"
                    dve.wait_ge(e3_ready, 1)
                    V.tensor_scalar(s3[:, :], s3[:, :], 0.5, 0.5, ALU.mult, ALU.add).then_inc(s3_ready, 1)
                    yield "hwgate"
                    dve.wait_ge(s3_tr, 1)
                    seq.link(V.tensor_copy(s3t[:, 0, :], F[0:PAIRS, 0, 0:P]))
                    V.tensor_copy(s3t[:, 2, :], s3t[:, 0, :])
                    V.tensor_tensor(s3t[:, 1, :], F[0:PAIRS, 0, 0:P], s3t[:, 0, :], ALU.subtract).then_inc(s3_split, 1)
                    yield "hwrows"
                    for i in range(4):
                        yield f"band{i}"
                    yield "bandcopy"
                    dve.wait_ge(e12_ready, 2)
                    V.tensor_scalar(s12[:, :, :, :], s12[:, :, :, :], 0.5, 0.5, ALU.mult, ALU.add).then_inc(s12_ready, 1)
                    yield "bandturn"
                    for k in range(NCH):
                        dve.wait_ge(s3b_done, k + 1)
                        if k:
                            dve.wait_ge(s3b_used, k)
                        else:
                            dve.wait_ge(y_tr, 1)
                        for t in range(CT):
                            last = V.tensor_tensor_reduce(out=junk[t], in0=F[:, k % 2, :], in1=Gn[:, t, chunk(2 * k)[2]],
                                                          scale=1.0, scalar=0.0, op0=ALU.mult, op1=ALU.add,
                                                          accum_out=part[:, t, k:k + 1])
                        last.then_inc(s3b_used, 1)
                        yield f"hwmean{k}"
                    dve.wait_ge(s3b_used, NCH)
                    dve.wait_ge(s12_ready, 1)
                    for t in range(CT):
                        V.tensor_tensor_reduce(out=junk[t][:, 0:2 * W].rearrange("p (m w) -> p m w", m=2),
                                               in0=s12[:, t, :, :], in1=Zv[:, t, :, 1, PAD:PAD + W], scale=1.0,
                                               scalar=0.0, op0=ALU.mult, op1=ALU.add, accum_out=sm[:, 0, t:t + 1])
                    seq.link(V.reduce_sum(sm[:, 1, :], part[:, :, :], AX.X))
                    seq.link(V.tensor_scalar(sm[:, 1, :], sm[:, 1, :], 1.0 / (3 * HW), None, ALU.mult))
                    V.scalar_tensor_tensor(pooled[:, :], sm[:, 0, :], 1.0 / (3 * W), sm[:, 1, :],
                                           ALU.mult, ALU.add).then_inc(pooled_set, 1)
                    yield "logits"
                    dve.wait_ge(logits_done, 1)
                    logits = F[:, 0, 0:3 * CT].rearrange("p (t k) -> p t k", k=3)
                    seq.link(V.reduce_max(sm[:, 2, :], logits, AX.X))
                    V.tensor_tensor(wt[:, :, :], logits, sm[:, 2, :].unsqueeze(2).to_broadcast([P, CT, 3]),
                                    ALU.subtract).then_inc(lg_ready, 1)
                    dve.wait_ge(lg_exp, 1)
                    seq.link(V.reduce_sum(sm[:, 0, :], wt[:, :, :], AX.X))
                    seq.link(V.reciprocal(sm[:, 1, :], sm[:, 0, :]))
                    seq.link(V.tensor_tensor(wt[:, :, :], wt[:, :, :], sm[:, 1, :].unsqueeze(2).to_broadcast([P, CT, 3]),
                                             ALU.mult))
                    for t in range(CT):
                        for m in range(2):
                            V.tensor_scalar(ab[:, t, W * m:W * m + W], s12[:, t, m, :], wt[:, t, m:m + 1], None, ALU.mult)
                    seq.link(V.tensor_copy(w3h[:, :], wt[:, :, 2]))
                    V.tensor_copy(w3c[:, :, 0], w3h[:, :])
                    V.tensor_copy(w3c[:, :, 1], w3h[:, :])
                    V.tensor_tensor(w3c[:, :, 2], wt[:, :, 2], w3h[:, :], ALU.subtract).then_inc(ab_set, 1)
                    yield "mix"
                    dve.wait_ge(ab_hi_set, 2)
                    V.tensor_tensor(ab_lo[:, :], F[:, 0, 0:C], ab_hi[:, :], ALU.subtract).then_inc(ab_lo_set, 1)
                    yield "mixturn"
                    for n in range(CT * NCH + 2):
                        if n < CT * NCH:
                            k, t, px = chunk(n)
                            dve.wait_ge(gate_done, n + 1)
                            V.tensor_tensor(Gn[:, t, px], Gn[:, t, px], F[:, n % 2, :], ALU.mult).then_inc(gated, 1)
                        if n >= 2:
                            dve.wait_ge(x1_set, n - 1)
                            last = chunk_stats(n - 2)
                        if n == CT * NCH + 1:
                            seq.link(last)
                            moments().then_inc(gn_stats, 1)
                        yield f"gate{n}"
                    norm_a(1)
                    yield "norm1a"
                    norm_b(1)
                    yield "norm1b"
                    norm_c(1)
                    yield "norm1c"
                    for n in range(4):
                        low_half(n)
                        yield f"split{n}"
                    for n in range(CT * NCH):
                        for i in range(6):
                            if i == 0 and n:
                                add_conv(n - 1)
                            if i == 1 and n + 4 < CT * NCH:
                                low_half(n + 4)
                            if i == 2 and n:
                                row_sums(n - 1)
                            yield f"conv{n}.{i}"
                    add_conv(CT * NCH - 1)
                    row_sums(CT * NCH - 1)
                    dve.wait_ge(dwt_used, CT * NCH)
                    moments().then_inc(gn_stats, 1)
                    for t in range(CT):
                        V.tensor_tensor_reduce(out=junk[t][:, 0:H], in0=y1[:, t, :], in1=uw[:, :], scale=1.0,
                                               scalar=0.0, op0=ALU.mult, op1=ALU.add, accum_out=ysum[:, 0, t:t + 1])
                    norm_a(2)
                    yield "norm2a"
                    norm_b(2)
                    yield "norm2b"
                    norm_c(2)
                    yield "norm2c"
                    dve.wait_ge(gn_coef, 3)
                    seq.link(V.tensor_tensor(ysum[:, 0, :], ysum[:, 0, :], g_r, ALU.mult))
                    V.scalar_tensor_tensor(ysum[:, 1, :], g_b, u_sum * u_sum, ysum[:, 0, :],
                                           ALU.mult, ALU.add).then_inc(se_y, 1)
                    dve.wait_ge(se_h, 1)
                    V.tensor_scalar(hid[:, :], F[0:HID, 0, 0:1], 0.0, None, ALU.max).then_inc(se_relu, 1)
                    yield "squeeze"
                    dve.wait_ge(se_exp, 1)
                    seq.link(V.tensor_scalar(wch[:, 0, :], wch[:, 0, :], 0.5, 0.5, ALU.mult, ALU.add))
                    V.tensor_tensor(beta, wch[:, 0, :], g_b, ALU.mult)
                    seq.link(V.tensor_tensor(alpha, wch[:, 0, :], g_r, ALU.mult))
                    seq.link(V.tensor_scalar(alpha, alpha, 1.0, None, ALU.add))
                    seq.link(V.tensor_tensor(mv[:, :, 0], mv[:, :, 0], alpha, ALU.mult))
                    V.tensor_tensor(mv[:, :, 0], mv[:, :, 0], beta, ALU.add)
                    seq.link(V.tensor_tensor(mv[:, :, 1], mv[:, :, 1], alpha, ALU.mult))
                    V.tensor_tensor(mv[:, :, 1], mv[:, :, 1], alpha, ALU.mult).then_inc(gn_stats, 1)
                    dve.wait_ge(gn_stats, 4)
                    yield "excite"
                    norm_a(3)
                    yield "norm3a"
                    norm_b(3)
                    yield "norm3b"
                    norm_c(3)
                    yield "norm3c"
                    if has_att:
                        dve.wait_ge(tok_hi_set, CT * NW)
                        dve.wait_ge(x3_set, CT * NW)
                    dve.wait_ge(gn_coef, 4)
                    V.tensor_tensor(c_a3, alpha, g_r, ALU.mult)
                    seq.link(V.tensor_tensor(b3, beta, g_r, ALU.mult))
                    V.tensor_tensor(c_b3, b3, g_b, ALU.add)
                    V.tensor_copy(c_alpha, alpha)
                    V.tensor_tensor(c_beta, beta, bvo[:, :], ALU.add)
                    yield "coefs"

                def low_half(n):
                    k, t, px = chunk(n)
                    dve.wait_ge(nrm_set, n + 1)
                    dve.wait_ge(hi_set, n + 1)
                    rows = slice(1 + ROWS * k, 1 + ROWS * k + ROWS)
                    V.tensor_tensor(halves[:, 1, t, rows, 1:1 + W], rows_view(tmp[:, n % 2, :]),
                                    halves[:, 0, t, rows, 1:1 + W], ALU.subtract).then_inc(lo_set, 1)

                def add_conv(n):
                    k, t, px = chunk(n)
                    dve.wait_ge(conv_done, n + 1)
                    V.scalar_tensor_tensor(X[:, t, px], F[:, n % 2, :], conv_inv, X[:, t, px], ALU.mult,
                                           ALU.add).then_inc(x2_set, 1)

                def row_sums(n):
                    k, t, px = chunk(n)
                    dve.wait_ge(x2_set, n + 1)
                    chunk_stats(n)
                    dve.wait_ge(dwt_mul, n + 1)
                    V.tensor_reduce(y1[:, t, ROWS * k:ROWS * k + ROWS], rows_view(tmp[:, 2 + n % 2, :]), AX.X,
                                    ALU.add).then_inc(dwt_used, 1)

                def low_tokens(r, t):
                    dve.wait_ge(tok_hi_set, CT * r + t + 1)
                    if r:
                        dve.wait_ge(qp_done, FILL[f"v1.{r - 1}"] + 1)
                    V.tensor_tensor(tok_lo[:, t, :].rearrange("p (w i j) -> p w i j", w=NW, i=WS),
                                    tok[:, t, :].rearrange("p (i w j) -> p w i j", w=NW, i=WS),
                                    tok_hi[:, t, :].rearrange("p (w i j) -> p w i j", w=NW, i=WS),
                                    ALU.subtract).then_inc(tok_lo_set, 1)

                def scores(u):
                    r, quad, hs, buf = u // 4, u // 2 % 2, u % 2, u % 4
                    dve.wait_ge(s_done, u + 1)
                    if u >= 4:
                        dve.wait_ge(pt_done, u - 3)
                    low = 2 * (r == NW - 1)

                    def add_bias(w0, w1_, kind):
                        span = slice(w0, w1_)
                        return V.tensor_tensor(
                            sc[:, buf, :].rearrange("p (g w m) -> p g w m", g=CT, w=4)[:, :, span, :],
                            SP[:, hs, :].rearrange("p (g w m) -> p g w m", g=CT, w=4)[:, :, span, :],
                            bias[:, kind, hs, :, :].unsqueeze(2).to_broadcast([P, CT, w1_ - w0, TOK]), ALU.add)

                    if quad == 0:
                        add_bias(0, 4, low).then_inc(s_biased, 1)
                    else:
                        add_bias(0, 3, low)
                        add_bias(3, 4, low + 1).then_inc(s_biased, 1)
                    dve.wait_ge(s_biased, u + 1)
                    V.tensor_reduce(mx[:, buf, :], keyed(sc[:, buf, :]), AX.X, ALU.max).then_inc(s_max, 1)

                def total(u):
                    dve.wait_ge(p_exp, u + 1)
                    seq.link(V.tensor_reduce(sums[:, u % 4, :], keyed(sc[:, u % 4, :]), AX.X, ALU.add))
                    V.reciprocal(rec[:, u % 4, :], sums[:, u % 4, :]).then_inc(p_rec, 1)

                def add_attention(r, co):
                    dve.wait_ge(qp_done, FILL[f"p{co}.{r}"] + 1)
                    dve.wait_ge(x3_set, CT * r + co + 1)
                    img = rows_view(xr[:, r % 3, co, :])
                    win = QP[:, :].rearrange("p (w i j) -> p w i j", w=NW, i=WS)

                    def piece(w0, w1_, j0, j1, col):
                        dst = img[:, :, col:col + (w1_ - w0) * (j1 - j0)].rearrange("p i (w j) -> p w i j", j=j1 - j0)
                        return V.tensor_tensor(dst, dst, win[:, w0:w1_, :, j0:j1], ALU.add)

                    piece(0, NW - 1, 0, WS, SHIFT)
                    piece(NW - 1, NW, 0, SHIFT, W - SHIFT)
                    last = piece(NW - 1, NW, SHIFT, WS, 0)
                    last.then_inc(qp_read, 1)
                    dve.wait_ge(qp_read, FILL[f"p{co}.{r}"] + 1)
                    V.memset(sm[:, 3, :], 0.0).then_inc(x4_set, 1)

                def att():
                    for name in ATT:
                        c, r = name[0], int(name[1:])
                        u, more = 4 * r, r + 1 < NW
                        if c == "p" and r < CT:
                            low_tokens(0, r)
                        if c in "CDEF":
                            scores(u + "CDEF".index(c))
                        if c in "EFGH":
                            total(u + "EFGH".index(c))
                        if c in "EF" and r:
                            add_attention(r - 1, "EF".index(c))
                        if c in "FG" and more:
                            low_tokens(r + 1, "FG".index(c))
                        if c in "LM":
                            add_attention(r, "LM".index(c))
                        yield name

                play(order, front(), att())

            @block.tensor
            def _(pe):
                def norm_mean(n):
                    pe.wait_ge(gn_stats, n + 1)
                    T.matmul(F[:, 0, 0:CT], gavg[:, :], mv[:, :, 0], start=True, stop=True).then_inc(gn_mean, 1)

                def norm_var(n):
                    pe.wait_ge(gn_sq, n + 1)
                    T.matmul(F[:, 1, 0:CT], gavg[:, :], g_sq, start=True, stop=True).then_inc(gn_var, 1)

                def band(i):
                    m, t = divmod(i, 2)
                    if t == 0:
                        T.matmul(F[0:W, m, 0:C + 2 * PAD], zrow[:, 0:W], zrow[:, :], start=True, stop=False,
                                 skip_group_check=True)
                    for j in range(NM):
                        last = T.matmul(F[0:W, m, P * t:P * t + BAND], Zv[:, t, m, j // KS, j % KS:j % KS + W],
                                        toep[:, m, j, :], start=False, stop=(t == CT - 1 and j == NM - 1),
                                        skip_group_check=True)
                    if t == CT - 1:
                        last.then_inc(y_done, 1)

                def front():
                    for i in range(4):
                        yield f"stats{i}"
                    norm_mean(0)
                    yield "norm0a"
                    norm_var(0)
                    yield "norm0b"
                    yield "norm0c"
                    for i in range(8):
                        for jj in (2 * i, 2 * i + 1):
                            if jj % (PAIRS // 8) == 0:
                                pe.wait_ge(g_ready, CT * (jj // (PAIRS // 8) + 1))
                            if jj >= 2:
                                pe.wait_ge(f_max, jj - 1)
                                pe.wait_ge(f_sum, jj - 1)
                            else:
                                pe.wait_ge(gn_ve, 1)
                            for j in (2 * jj, 2 * jj + 1):
                                for t in range(CT):
                                    last = T.transpose(F[:, jj % 2, C * (j % 2) + P * t:C * (j % 2) + P * t + P],
                                                       Gn[:, t, P * j:P * j + P], ident[:, :])
                            last.then_inc(f_tr, 1)
                        yield f"reduce{i}"
                    yield "zpool"
                    pe.wait_ge(f_max, PAIRS // 2)
                    pe.wait_ge(f_sum, PAIRS // 2)
                    for i in range(2 * DJ):
                        ch, dj = divmod(i, DJ)
                        last = T.matmul(F[:, 1, 0:PAIRS], t_hw[:, i, :, :].rearrange("p a w -> p (a w)"),
                                        Z3[:, ch, dj:dj + PAIRS], start=(i == 0), stop=(i == 2 * DJ - 1))
                    last.then_inc(y3_done, 1)
                    yield "hwconv"
                    yield "hwgate"
                    pe.wait_ge(s3_ready, 1)
                    T.transpose(F[0:PAIRS, 0, 0:P], s3[:, :], ident[:, :]).then_inc(s3_tr, 1)
                    yield "hwrows"
                    pe.wait_ge(z_ready, 1)
                    pe.wait_ge(s3_split, 1)
                    for i in range(4):
                        band(i)
                        yield f"band{i}"
                    pe.wait_ge(y_copied, 2)
                    yield "bandcopy"
                    for t in range(CT):
                        for m in range(2):
                            last = T.transpose(F[:, 0, W * (2 * t + m):W * (2 * t + m) + W], yt[:, m, P * t:P * t + P],
                                               ident[0:W, 0:W])
                    last.then_inc(y_tr, 1)
                    yield "bandturn"
                    pe.wait_ge(srow_in, 48)
                    pe.wait_ge(e12_ready, 2)
                    for k in range(NCH):
                        if k >= 2:
                            pe.wait_ge(s3b_used, k - 1)
                        T.matmul(F[:, k % 2, :], ones3[:, :], srow[:, CHUNK * k:CHUNK * k + CHUNK], start=True,
                                 stop=True).then_inc(s3b_done, 1)
                        yield f"hwmean{k}"
                    pe.wait_ge(pooled_set, 1)
                    for to in range(CT):
                        for k in range(3):
                            for ti in range(CT):
                                lo = P * (to - ti + 1)
                                last = T.matmul(F[:, 0, 3 * to + k:3 * to + k + 1], t_1d[:, k, lo:lo + P],
                                                pooled[:, ti:ti + 1], start=(ti == 0), stop=(ti == CT - 1))
                    last.then_inc(logits_done, 1)
                    yield "logits"
                    yield "mix"
                    pe.wait_ge(ab_set, 1)
                    for t in range(CT):
                        T.transpose(F[:, 0, P * t:P * t + P], ab[:, t, :], ident[:, :])
                        last = T.transpose(F[0:3, 1, P * t:P * t + P], w3c[:, t, :], ident[:, :])
                    last.then_inc(ab_tr, 1)
                    yield "mixturn"
                    pe.wait_ge(ab_hi_set, 2)
                    pe.wait_ge(ab_lo_set, 1)
                    for n in range(CT * NCH + 2):
                        if n < CT * NCH:
                            k, t, px = chunk(n)
                            if n >= 2:
                                pe.wait_ge(gated, n - 1)
                            T.matmul(F[:, n % 2, :], ab_hi[:, P * t:P * t + P], ind[:, px], start=True, stop=False)
                            T.matmul(F[:, n % 2, :], ab_lo[:, P * t:P * t + P], ind[:, px], start=False, stop=False)
                            T.matmul(F[:, n % 2, :], w3t[:, P * t:P * t + P], srow[:, px], start=False,
                                     stop=True).then_inc(gate_done, 1)
                        yield f"gate{n}"
                    norm_mean(1)
                    yield "norm1a"
                    norm_var(1)
                    yield "norm1b"
                    yield "norm1c"
                    for n in range(4):
                        yield f"split{n}"
                    for n in range(CT * NCH):
                        k, co = divmod(n, CT)
                        if co == 0:
                            pe.wait_ge(lo_set, CT * min(k + 2, NCH))
                        if n >= 2:
                            pe.wait_ge(x2_set, n - 1)
                        for i in range(6):
                            ci, third = divmod(i, 3)
                            for tap in range(3 * third, 3 * third + 3):
                                dy, dx = divmod(tap, C3)
                                win = [halves[:, l, ci, ROWS * k + dy:ROWS * k + dy + ROWS, dx:dx + W] for l in range(2)]
                                for j, (wgt, which) in enumerate(((cw_hi, 0), (cw_hi, 1), (cw_lo, 0))):
                                    last = T.matmul(F[:, n % 2, :], wgt[:, ci, tap, P * co:P * co + P], win[which],
                                                    start=(ci == 0 and tap == 0 and j == 0),
                                                    stop=(ci == CT - 1 and tap == TAPS - 1 and j == 2))
                            if i == 5:
                                last.then_inc(conv_done, 1)
                            yield f"conv{n}.{i}"
                    pe.wait_ge(x2_set, CT * NCH)
                    norm_mean(2)
                    yield "norm2a"
                    norm_var(2)
                    yield "norm2b"
                    yield "norm2c"
                    pe.wait_ge(se_y, 1)
                    for t in range(CT):
                        last = T.matmul(F[0:HID, 0, 0:1], w1[:, t, :], ysum[:, 1, t:t + 1], start=(t == 0),
                                        stop=(t == CT - 1))
                    last.then_inc(se_h, 1)
                    yield "squeeze"
                    pe.wait_ge(se_relu, 1)
                    for t in range(CT):
                        last = T.matmul(F[:, 1, t:t + 1], w2[:, P * t:P * t + P], hid[:, :], start=True, stop=True)
                    last.then_inc(se_z, 1)
                    yield "excite"
                    norm_mean(3)
                    yield "norm3a"
                    norm_var(3)
                    yield "norm3b"
                    yield "norm3c"
                    yield "coefs"

                HALVES = ((qkv_hi, tok_hi), (qkv_hi, tok_lo), (qkv_lo, tok_hi))

                def fill(name):
                    kind, r = name.split(".")
                    r, i = int(r), int(kind[1])
                    if FILL[name]:
                        pe.wait_ge(qp_read, FILL[name])
                    if kind[0] in "qk":
                        if kind == "q0":
                            pe.wait_ge(tok_lo_set, CT * (r + 1))
                        oc = i + 2 * (kind[0] == "k")
                        for j in range(6):
                            ci, (wgt, tk) = j // 3, HALVES[j % 3]
                            last = T.matmul(QP[:, :], wgt[:, ci, P * oc:P * oc + P], tk[:, ci, :],
                                            start=(j == 0), stop=(j == 5))
                    elif kind[0] == "v":
                        for b in range(2):
                            lo = P * (2 * i + b)
                            for j in range(6):
                                ci, (wgt, tk) = j // 3, HALVES[j % 3]
                                last = T.matmul(QP[:, C * b:C * b + C], tk[:, ci, lo:lo + P], wgt[:, ci, 2 * C:3 * C],
                                                start=(j == 0), stop=(j == 5))
                    else:
                        pe.wait_ge(o_read, r + 1)
                        for ci in range(CT):
                            last = T.matmul(QP[:, :], wo[:, ci, P * i:P * i + P], ot[:, ci, :],
                                            start=(ci == 0), stop=(ci == CT - 1))
                    last.then_inc(qp_done, 1)

                def scores(u):
                    r, quad, hs = u // 4, u // 2 % 2, u % 2
                    if u >= 2:
                        pe.wait_ge(s_biased, u - 1)
                    if u % 4 == 0:
                        pe.wait_ge(qp_read, FILL[f"k1.{r}"] + 1)
                    rows = slice(64 * hs, 64 * hs + 64)
                    for cg in range(CT):
                        for w in range(4):
                            win = 4 * quad + w
                            last = T.matmul(SP[:, hs, 256 * cg + TOK * w:256 * cg + TOK * w + TOK],
                                            qbd[rows, cg, win, :, :].rearrange("p h n -> p (h n)"),
                                            kk[rows, cg, TOK * win:TOK * win + TOK], start=True, stop=True)
                    last.then_inc(s_done, 1)

                def turn_probs(u):
                    pe.wait_ge(p_norm, u + 1)
                    if u:
                        pe.wait_ge(pt_read, u)
                    for b in range(4):
                        last = T.transpose(PTR[:, P * b:P * b + P], sc[:, u % 4, P * b:P * b + P], ident[:, :])
                    last.then_inc(pt_done, 1)

                def weigh(u):
                    r, quad, hs = u // 4, u // 2 % 2, u % 2
                    pe.wait_ge(pt_read, u + 1)
                    if u % 4 == 0:
                        pe.wait_ge(qp_read, FILL[f"v1.{r}"] + 1)
                        if r:
                            pe.wait_ge(o_read, r)
                    for b in range(4):
                        cg, wp = divmod(b, 2)
                        pair = 2 * quad + wp
                        for h2 in range(2):
                            h = 4 * cg + 2 * hs + h2
                            for par in range(2):
                                rows = slice(64 * par, 64 * par + 64)
                                cols = 256 * cg + TOK * pair
                                last = T.matmul(O[DH * (h % 4):DH * (h % 4) + DH, par, cols:cols + TOK],
                                                vv[rows, pair, DH * h:DH * h + DH],
                                                prt[rows, u % 2, P * b + TOK * h2:P * b + TOK * h2 + TOK],
                                                start=True, stop=True)
                    last.then_inc(pv_done, 1)

                def att():
                    for name in ATT:
                        c, r = name[0], int(name[1:])
                        u, more = 4 * r, r + 1 < NW
                        if c == "p" and r >= 2:
                            fill(FILLS[r - 2])
                        if c in "CDEF":
                            scores(u + "CDEF".index(c))
                        if c in "CD":
                            fill(f"v{'CD'.index(c)}.{r}")
                        if c in "EF" and r:
                            fill(f"p{'EF'.index(c)}.{r - 1}")
                        if c in "GHIJ":
                            turn_probs(u + "GHIJ".index(c))
                        if c in "HIJK":
                            if more:
                                fill(("q0", "q1", "k0", "k1")["HIJK".index(c)] + f".{r + 1}")
                            weigh(u + "HIJK".index(c))
                        if c in "LM":
                            fill(f"p{'LM'.index(c)}.{r}")
                        yield name

                play(order, front(), att())

        clear_semaphores()
        with nc.Block() as block:
            @block.sync
            def _(sp):
                for t in range(CT):
                    sp.dma_start(X[:, t, :], x[0, P * t:P * t + P, :]).then_inc(x_loaded, 16)
                sp.wait_ge(x_loaded, 16 * CT)
        turn(0, None, 1)
        clear_semaphores()
        if NB > 2:
            with nc.Fori(1, NB - 1) as image:
                turn(image, image - 1, image + 1)
                clear_semaphores()
        turn(NB - 1, NB - 2, None)
        clear_semaphores()
        turn(None, NB - 1, None)


def shift_mask():
    img = np.zeros((H, W), np.int32)
    cnt = 0
    for hs in (slice(0, -WS), slice(-WS, -SHIFT), slice(-SHIFT, None)):
        for ws_ in (slice(0, -WS), slice(-WS, -SHIFT), slice(-SHIFT, None)):
            img[hs, ws_] = cnt
            cnt += 1
    mw = img.reshape(NW, WS, NW, WS).transpose(0, 2, 1, 3).reshape(NW, NW, TOK)
    kinds = np.stack([mw[0, 0], mw[0, -1], mw[-1, 0], mw[-1, -1]])
    mask = np.where(kinds[:, :, None] != kinds[:, None, :], -100.0, 0.0).astype(np.float32)
    return np.concatenate([mask.transpose(1, 0, 2)] * 2, axis=0)


def constants():
    gavg = np.kron(np.eye(P // GROUP), np.ones((GROUP, GROUP)) / GROUP).astype(np.float32)
    ind = np.zeros((P, H, W), np.float16)
    ind[np.arange(W), :, np.arange(W)] = 1
    ind[W + np.arange(H), np.arange(H), :] = 1
    ones3 = np.zeros((3, P), np.float16)
    ones3[0:2] = 1
    half = np.zeros((P, 2), np.float32)
    half[np.arange(P), np.arange(P) // DH % 2] = 1
    return {"c_gavg": gavg, "c_ident": np.eye(P, dtype=np.float32), "c_ind": ind.reshape(P, HW),
            "c_ones3": ones3, "c_mask": shift_mask(), "c_u": dwt_mean_weights(W).astype(np.float32), "c_half": half}


def kernel(**inputs):
    import concourse.bacc as _bacc
    from concourse.bass_utils import run_bass_kernel_spmd as _run

    a = {k: np.asarray(v) for k, v in inputs.items()}
    names = ("cw", "hc", "hw")
    bn = np.stack([np.concatenate([a[f"L0_conv_{q}_{n}"] for n in names]) for q in "gbmv"])
    arrays = {
        "x": a["x"].reshape(NB, C, HW),
        "k_cw": a["L0_conv_w_cw"][0].transpose(0, 2, 1)[:, :, ::-1],
        "k_hc": a["L0_conv_w_hc"][0][:, :, ::-1],
        "k_hw": a["L0_conv_w_hw"][0][:, :, ::-1],
        "bn": bn,
        "k_1d": a["L0_conv_w1d"][:, 0, ::-1],
        "w_conv": a["L1_conv_weight"].reshape(C, C * TAPS),
        "alphas": a["L1_conv_alphas"],
        "w1t": a["L2_conv_W1"].T,
        "w2t": a["L2_conv_W2"].T,
        "w_qkv": a["L3_conv_w_qkv"],
        "b_qkv": a["L3_conv_b_qkv"].reshape(-1, P).T,
        "w_o": a["L3_conv_w_o"],
        "b_o": a["L3_conv_b_o"].reshape(-1, P).T,
        "rel_t": a["L3_conv_rel_bias_table"].T,
        **constants(),
    }
    nc = _bacc.Bacc("TRN2", target_bir_lowering=False, num_devices=1)
    feed, args = {}, []
    for name, v in arrays.items():
        v = np.ascontiguousarray(v)
        feed[f"in_{name}"] = v
        args.append(nc.dram_tensor(f"in_{name}", v.shape, mybir.dt.from_np(v.dtype), kind="ExternalInput").ap())
    out = nc.dram_tensor("out_x", (NB, C, HW), mybir.dt.float32, kind="ExternalOutput").ap()
    build(nc, *args, out)
    r = _run(nc, [feed], core_ids=[0])
    return r.results[0]["out_x"].reshape(NB, C, H, W)
```
